# Optimizing a Trainium2 kernel written in Bass

```python
import numpy as np
import jax
import jax.numpy as jnp

def _softmax(x, axis=-1):
    return jax.nn.softmax(x, axis=axis)

def _gelu(x):
    return jax.nn.gelu(x, approximate=True)

def _silu(x):
    return jax.nn.silu(x)

def _sigmoid(x):
    return jax.nn.sigmoid(x)

def _layernorm(x, axis=-1, eps=1e-05):
    m = jnp.mean(x, axis=axis, keepdims=True)
    v = jnp.var(x, axis=axis, keepdims=True)
    return (x - m) / jnp.sqrt(v + eps)

def _scatter_add(tgt, idx, src, axis=0):
    return tgt.at[idx].add(src)

def _segment_sum(src, seg, n):
    return jax.ops.segment_sum(src, seg, n)
kernel_name = 'mk_seq_postln_d1_jaxref_r8_03d467'

def setup_inputs(seed: int=0):
    np.random.seed(seed)
    _w = jnp.asarray

    def _L0_attn_setup():
        import jax, jax.numpy as jnp
        import numpy as np
        D_MODEL = 128
        D_INNER = 128
        N_HEADS = 16
        HEAD_DIM = D_INNER // N_HEADS
        D_STATE = 16
        DT_RANK = 16
        CHUNK = 64
        PROJ = 2 * D_INNER + 2 * D_STATE * N_HEADS + DT_RANK

        def _forward(x, W_in, dt_W, dt_b, A_log, D_param, W_out, norm_w):
            B, S, _ = x.shape
            H, P, N, K = (N_HEADS, HEAD_DIM, D_STATE, CHUNK)
            proj = x @ W_in.T
            xp = proj[..., :D_INNER]
            z = proj[..., D_INNER:2 * D_INNER]
            o = 2 * D_INNER
            B_ssm = proj[..., o:o + N * H].reshape(B, S, H, N)
            C_ssm = proj[..., o + N * H:o + 2 * N * H].reshape(B, S, H, N)
            dt_low = proj[..., o + 2 * N * H:]
            dt = jax.nn.softplus(dt_low @ dt_W.T + dt_b)
            xp = xp.reshape(B, S, H, P)
            A = -jnp.exp(A_log)
            nC = S // K
            xc = xp.reshape(B, nC, K, H, P)
            dtc = dt.reshape(B, nC, K, H)
            Bc = B_ssm.reshape(B, nC, K, H, N)
            Cc = C_ssm.reshape(B, nC, K, H, N)
            dA = dtc * A
            dAcs = jnp.cumsum(dA, axis=2)
            Lm = jnp.exp(dAcs[:, :, :, None, :] - dAcs[:, :, None, :, :])
            causal = jnp.tril(jnp.ones((K, K), jnp.float32))
            Lm = Lm * causal[None, None, :, :, None]
            scores = jnp.einsum('bcihn,bcjhn->bcijh', Cc, Bc) * Lm * dtc[:, :, None, :, :]
            y_intra = jnp.einsum('bcijh,bcjhp->bcihp', scores, xc)
            decay_to_end = jnp.exp(dAcs[:, :, -1:, :] - dAcs)
            wx = (dtc * decay_to_end)[..., None] * xc
            chunk_state = jnp.einsum('bckhn,bckhp->bchnp', Bc, wx)
            chunk_decay = jnp.exp(dAcs[:, :, -1, :])

            def step(h, inp):
                d, s = inp
                return (d[:, :, None, None] * h + s, h)
            h0 = jnp.zeros((B, H, N, P), jnp.float32)
            _, h_states = jax.lax.scan(step, h0, (jnp.moveaxis(chunk_decay, 1, 0), jnp.moveaxis(chunk_state, 1, 0)))
            h_states = jnp.moveaxis(h_states, 0, 1)
            y_cross = jnp.einsum('bcthn,bchnp,bcth->bcthp', Cc, h_states, jnp.exp(dAcs))
            y = (y_intra + y_cross).reshape(B, S, H, P)
            y = y + xp * D_param[None, None, :, None]
            y = y.reshape(B, S, D_INNER)
            rms = jnp.sqrt(jnp.mean(y * y, axis=-1, keepdims=True) + 1e-06)
            y = y / rms * norm_w
            y = y * jax.nn.silu(z)
            return y @ W_out.T
        key = jax.random.key(seed)
        ks = jax.random.split(key, 6)
        B, S = (4, 512)
        x = jax.random.normal(ks[0], (B, S, D_MODEL), jnp.float32)
        W_in = jax.random.normal(ks[1], (PROJ, D_MODEL), jnp.float32) * 0.02
        dt_W = jax.random.normal(ks[2], (N_HEADS, DT_RANK), jnp.float32) * 0.1
        dt_b = jax.random.normal(ks[3], (N_HEADS,), jnp.float32) * 0.1
        A_log = jnp.full((N_HEADS,), jnp.log(0.5), jnp.float32)
        D_param = jnp.ones((N_HEADS,), jnp.float32)
        W_out = jax.random.normal(ks[4], (D_MODEL, D_INNER), jnp.float32) * 0.02
        norm_w = jnp.ones((D_INNER,), jnp.float32)
        return dict(x=x, W_in=W_in, dt_W=dt_W, dt_b=dt_b, A_log=A_log, D_param=D_param, W_out=W_out, norm_w=norm_w)
    _L0_attn_in = _L0_attn_setup()

    def _L0_ffn_setup():
        import jax, jax.numpy as jnp
        import numpy as np
        B, L, D = (4, 64, 128)
        E, TOP_K = (16, 4)
        F = 4 * D
        key = jax.random.key(seed)
        ks = jax.random.split(key, 6)
        scale = 0.02
        return {'x': jax.random.normal(ks[0], (B, L, D), jnp.float32), 'keys': jax.random.normal(ks[1], (E, D), jnp.float32), 'w1': jax.random.normal(ks[2], (E, F, D), jnp.float32) * scale, 'b1': jnp.zeros((E, F), jnp.float32), 'w2': jax.random.normal(ks[3], (E, D, F), jnp.float32) * scale, 'b2': jnp.zeros((E, D), jnp.float32), 'rw': jax.random.normal(ks[4], (E, D), jnp.float32) * scale, 'rb': jnp.zeros((E,), jnp.float32)}
    _L0_ffn_in = _L0_ffn_setup()
    _d = {'L0_attn_x': _L0_attn_in['x'], 'L0_attn_W_in': _L0_attn_in['W_in'], 'L0_attn_dt_W': _L0_attn_in['dt_W'], 'L0_attn_dt_b': _L0_attn_in['dt_b'], 'L0_attn_A_log': _L0_attn_in['A_log'], 'L0_attn_D_param': _L0_attn_in['D_param'], 'L0_attn_W_out': _L0_attn_in['W_out'], 'L0_attn_norm_w': _L0_attn_in['norm_w'], 'L0_ffn_keys': _L0_ffn_in['keys'], 'L0_ffn_w1': _L0_ffn_in['w1'], 'L0_ffn_b1': _L0_ffn_in['b1'], 'L0_ffn_w2': _L0_ffn_in['w2'], 'L0_ffn_b2': _L0_ffn_in['b2'], 'L0_ffn_rw': _L0_ffn_in['rw'], 'L0_ffn_rb': _L0_ffn_in['rb']}
    _x0 = _d['L0_attn_x']
    _d['L0_attn_x'] = jax.random.normal(jax.random.fold_in(jax.random.key(seed), 1), (1, 2048, 128), dtype=_x0.dtype)
    del _x0
    return _d

def reference(L0_attn_x, L0_attn_W_in, L0_attn_dt_W, L0_attn_dt_b, L0_attn_A_log, L0_attn_D_param, L0_attn_W_out, L0_attn_norm_w, L0_ffn_keys, L0_ffn_w1, L0_ffn_b1, L0_ffn_w2, L0_ffn_b2, L0_ffn_rw, L0_ffn_rb):

    def _L0_attn_ref(x, W_in, dt_W, dt_b, A_log, D_param, W_out, norm_w):
        import jax, jax.numpy as jnp
        import numpy as np
        D_MODEL = 128
        D_INNER = 128
        N_HEADS = 16
        HEAD_DIM = D_INNER // N_HEADS
        D_STATE = 16
        DT_RANK = 16
        CHUNK = 64
        PROJ = 2 * D_INNER + 2 * D_STATE * N_HEADS + DT_RANK

        def _forward(x, W_in, dt_W, dt_b, A_log, D_param, W_out, norm_w):
            B, S, _ = x.shape
            H, P, N, K = (N_HEADS, HEAD_DIM, D_STATE, CHUNK)
            proj = x @ W_in.T
            xp = proj[..., :D_INNER]
            z = proj[..., D_INNER:2 * D_INNER]
            o = 2 * D_INNER
            B_ssm = proj[..., o:o + N * H].reshape(B, S, H, N)
            C_ssm = proj[..., o + N * H:o + 2 * N * H].reshape(B, S, H, N)
            dt_low = proj[..., o + 2 * N * H:]
            dt = jax.nn.softplus(dt_low @ dt_W.T + dt_b)
            xp = xp.reshape(B, S, H, P)
            A = -jnp.exp(A_log)
            nC = S // K
            xc = xp.reshape(B, nC, K, H, P)
            dtc = dt.reshape(B, nC, K, H)
            Bc = B_ssm.reshape(B, nC, K, H, N)
            Cc = C_ssm.reshape(B, nC, K, H, N)
            dA = dtc * A
            dAcs = jnp.cumsum(dA, axis=2)
            Lm = jnp.exp(dAcs[:, :, :, None, :] - dAcs[:, :, None, :, :])
            causal = jnp.tril(jnp.ones((K, K), jnp.float32))
            Lm = Lm * causal[None, None, :, :, None]
            scores = jnp.einsum('bcihn,bcjhn->bcijh', Cc, Bc) * Lm * dtc[:, :, None, :, :]
            y_intra = jnp.einsum('bcijh,bcjhp->bcihp', scores, xc)
            decay_to_end = jnp.exp(dAcs[:, :, -1:, :] - dAcs)
            wx = (dtc * decay_to_end)[..., None] * xc
            chunk_state = jnp.einsum('bckhn,bckhp->bchnp', Bc, wx)
            chunk_decay = jnp.exp(dAcs[:, :, -1, :])

            def step(h, inp):
                d, s = inp
                return (d[:, :, None, None] * h + s, h)
            h0 = jnp.zeros((B, H, N, P), jnp.float32)
            _, h_states = jax.lax.scan(step, h0, (jnp.moveaxis(chunk_decay, 1, 0), jnp.moveaxis(chunk_state, 1, 0)))
            h_states = jnp.moveaxis(h_states, 0, 1)
            y_cross = jnp.einsum('bcthn,bchnp,bcth->bcthp', Cc, h_states, jnp.exp(dAcs))
            y = (y_intra + y_cross).reshape(B, S, H, P)
            y = y + xp * D_param[None, None, :, None]
            y = y.reshape(B, S, D_INNER)
            rms = jnp.sqrt(jnp.mean(y * y, axis=-1, keepdims=True) + 1e-06)
            y = y / rms * norm_w
            y = y * jax.nn.silu(z)
            return y @ W_out.T
        return _forward(x, W_in, dt_W, dt_b, A_log, D_param, W_out, norm_w)

    def _L0_ffn_ref(x, keys, w1, b1, w2, b2, rw, rb):
        import jax, jax.numpy as jnp
        import numpy as np
        B, L, D = (4, 64, 128)
        E, TOP_K = (16, 4)
        F = 4 * D
        diff = x[:, :, None, :] - keys
        dist2 = jnp.sum(diff * diff, axis=-1)
        logits = -dist2 + jnp.einsum('bld,ed->ble', x, rw) + rb
        topv, topi = jax.lax.top_k(logits, TOP_K)
        w = jax.nn.softmax(topv, axis=-1)
        hidden = jax.nn.gelu(jnp.einsum('bld,efd->blef', x, w1) + b1, approximate=False)
        exp_out = jnp.einsum('blef,edf->bled', hidden, w2) + b2
        sel = jnp.take_along_axis(exp_out, topi[..., None], axis=2)
        fused = jnp.sum(w[..., None] * sel, axis=2)
        return fused
    x = L0_attn_x
    x = _layernorm(x + _L0_attn_ref(x, L0_attn_W_in, L0_attn_dt_W, L0_attn_dt_b, L0_attn_A_log, L0_attn_D_param, L0_attn_W_out, L0_attn_norm_w), axis=-1)
    x = _layernorm(x + _L0_ffn_ref(x, L0_ffn_keys, L0_ffn_w1, L0_ffn_b1, L0_ffn_w2, L0_ffn_b2, L0_ffn_rw, L0_ffn_rb), axis=-1)
    return x

_drawn_inputs = setup_inputs


def setup_inputs(seed=0):
    import zlib

    import numpy as np

    out = dict(_drawn_inputs(seed))
    spreads = {'L0_attn_A_log': (-0.6931471824645996, 0.6),
     'L0_attn_D_param': (1.0, 0.6),
     'L0_attn_norm_w': (1.0, 0.6),
     'L0_ffn_b1': (0.0, 0.336),
     'L0_ffn_b2': (0.0, 0.1),
     'L0_ffn_rb': (0.0, 0.8)}
    factors = {'L0_attn_dt_W': 8.0, 'L0_attn_dt_b': 8.0, 'L0_ffn_rw': 8.0}
    for name, (base, spread) in spreads.items():
        noise = np.random.default_rng([zlib.crc32(name.encode()), seed]).standard_normal(out[name].shape)
        drawn = base * np.exp(spread * noise) if base else spread * noise
        out[name] = jnp.asarray(drawn.astype(out[name].dtype))
    for name, factor in factors.items():
        out[name] = (out[name] * factor).astype(out[name].dtype)
    return out
```

```python
from contextlib import ExitStack

import numpy as np

import concourse.bass as bass
from concourse import mybir

ALU = mybir.AluOpType
ACT = mybir.ActivationFunctionType
AX_X = mybir.AxisListType.X
F32 = mybir.dt.float32
BF16 = mybir.dt.bfloat16
I32 = mybir.dt.int32
U32 = mybir.dt.uint32

P = 128
D = 128
S = 2048
NT = S // P
H, HD, NS = 16, 8, 16
Q = 64
NC = P // Q
HH = H // 2
E, TOPK, F = 16, 4, 512
FB = F // P
NBLK = S * TOPK // P + E - 1
NBP = NBLK + 1
ROW = D + 3 * TOPK
RA, RI, RG = D, D + TOPK, D + 2 * TOPK
SKIP = float(4 * S * TOPK)
EPS_LN, EPS_RMS = 1e-5, 1e-6


class Step:

    def __init__(self, base, unroll, off, peeled):
        self.base, self.unroll, self.off, self.peeled = base, unroll, off, peeled

    def back(self, k):
        return Step(self.base, self.unroll, self.off - k, self.peeled)

    def val(self, mul=1, add=0):
        fixed = self.off * mul + add
        return fixed if self.peeled else self.base * (self.unroll * mul) + fixed

    def count(self):
        return self.val(1, 1)

    def slot(self, ring):
        return self.off % ring

    def dma(self, ring):
        turn = self.off // ring
        return 16 * (turn + 1) if self.peeled else self.base * (16 * (self.unroll // ring)) + 16 * (turn + 1)

    def live(self, n):
        return not self.peeled or 0 <= self.off < n

    def had(self, k):
        return not self.peeled or self.off >= k


def run_steps(eng, body, n, unroll, lo, last):
    hi = lo + (n - lo) // unroll * unroll
    for s in range(lo):
        body(Step(0, unroll, s, True))
    with eng.Fori(lo // unroll, hi // unroll) as i:
        for u in range(unroll):
            body(Step(i, unroll, u, False))
    for s in range(hi, last):
        body(Step(0, unroll, s, True))


def wait_apart(eng, waits, past, past_value):
    waits = [(sem, v if isinstance(v, int) else eng.to_reg(v)) for sem, v in waits]
    eng.wait_ge(past, past_value)
    for sem, v in waits:
        eng.wait_ge(sem, v)


def const_table():
    p = np.arange(P)[:, None]
    cols = {}
    cols["ident"] = np.eye(P)
    same = (p // Q) == (np.arange(P)[None] // Q)
    cols["decay"] = same * ((p <= np.arange(P)[None]) * 1.0 - 0.5)
    cols["chunk0"] = np.repeat((p < Q) * 1.0, P, 1)
    cols["chunk1"] = np.repeat((p >= Q) * 1.0, P, 1)
    cols["before"] = (p < np.arange(P)[None]) * 1.0
    cols["ones"] = np.ones((P, P))
    cols["causal"] = (p % Q <= np.arange(Q)[None]) * 1.0
    cols["head8"] = (p // NS == np.arange(HH)[None]) * 1.0
    cols["head16"] = (p // NS == np.arange(H)[None] % HH) * 1.0
    cols["eids"] = np.tile(np.arange(E), (P, TOPK)) * 1.0
    cols["ebase"] = np.tile(np.arange(E) * S, (P, 1)) * 1.0
    cols["tokid"] = (np.arange(NT)[None] * P + p)[:, :, None] * TOPK + np.arange(TOPK)[None, None] * 1.0
    cols["tokid"] = cols["tokid"].reshape(P, NT * TOPK)
    cols["part"] = p * 1.0
    cols["part128"] = p * 128.0
    cols["mhalf"] = np.full((P, 1), -0.5)
    at, out, n = {}, [], 0
    for k, v in cols.items():
        at[k] = (n, n + v.shape[1])
        n += v.shape[1]
        out.append(v.astype(np.float32))
    return at, np.ascontiguousarray(np.concatenate(out, 1))


SMALL = {"dt_b": (0, 16), "A_log": (16, 32), "D_param": (32, 48), "rb": (48, 64), "norm_w": (64, 65)}


def block_and_moe(nc, d, debug=None):
    at, _ = const_table()
    with ExitStack() as ctx:
        def sb(name, shape, dt=F32):
            return ctx.enter_context(nc.sbuf_tensor(name, shape, dt))

        def sem(name):
            return ctx.enter_context(nc.semaphore(name))

        def sems(name, n):
            return [sem(f"{name}{i}") for i in range(n)]

        cst = sb("cst", [P, at["mhalf"][1]])
        small = sb("small", [P, 65])
        dtlow = sb("dtlow", [16, D + 16])
        xT_all = sb("xT_all", [D, S])
        x_all = sb("x_all", [P, NT, D])
        winT = sb("winT", [D, 768])
        woutT = sb("woutT", [D, D])
        woutn = sb("woutn", [D, D])
        kT = sb("kT", [D, 2, E])
        kw = sb("kw", [D, E])
        ksq = sb("ksq", [D, E])
        kb = sb("kb", [P, E])
        w1s = sb("w1s", [D, E, F])
        w2s = sb("w2s", [P, E, FB, D])
        b1s = sb("b1s", [P, E, F])
        b2s = sb("b2s", [P, E, D])
        zrow = sb("zrow", [P, ROW])
        shared = sb("shared", [P, 8448])
        used = [0]

        def view(*shape):
            n = int(np.prod(shape))
            a = shared[:, used[0]:used[0] + n]
            used[0] += n
            if len(shape) > 1:
                names = " ".join("abcd"[:len(shape)])
                a = a.rearrange(f"p ({names}) -> p {names}", **dict(zip("abcd", shape)))
            return a

        wdt = sb("wdt", [D, H])
        dtu, dta, dte, dtl, dts, dA = (view(NT * H) for n in range(6))
        expA = sb("expA", [P, H])
        fC = sb("fC", [P, NT, H])
        fE = sb("fE", [P, NT * H])
        fB = sb("fB", [P, NT, H])
        ts, gs, gx = view(NT, NC, H), view(NT * NC, H), view(NT * NC, H)
        gm = sb("gm", [P, NT * NC, H])
        before = sb("before", [P, P], BF16)
        ones16 = sb("ones16", [P, P], BF16)

        def two(name, shape, dt=F32):
            return [sb(f"{name}{i}", shape, dt) for i in range(2)]

        used[0] = 0
        xT = two("xT", [D, P])
        cs, bs = two("cs", [P, H * NS]), two("bs", [P, H * NS])
        xz = two("xz", [P, NC, D])
        xd = two("xd", [P, D])
        z, ez, ez1, rz, sil = ([view(D), view(D)] for n in range(5))
        cb = [view(4, P), view(4, P)]
        cbd = [[view(NC, HH, Q) for j in range(2)] for i in range(2)]
        sc = [view(H, Q) for i in range(2)]
        st = two("st", [P, 2, D // 2])
        hs = two("hs", [P, NC, 2, D // 2])
        yr, ysq, yg, yT = (two(n, [P, D]) for n in ("yr", "ysq", "yg", "yT"))
        ss, ms, rs = (two(n, [P, 1]) for n in ("ss", "ms", "rs"))
        res = two("res", [P, D])
        bn = two("bn", [P, 6])
        mv, vre, rv = two("mv", [P, 2]), two("vre", [P, 1]), two("rv", [P, 1])
        rows = two("rows", [P, ROW])
        x2 = two("x2", [P, D])
        x2T, x2sq = two("x2T", [D, P]), two("x2sq", [P, D])
        xsq = two("xsq", [P, 1])
        x2_all = x_all
        lg = two("lg", [P, E])
        v8, i8 = two("v8", [P, 8]), two("i8", [P, 8], U32)
        nv, gsum, gr = two("nv", [P, 1]), two("gsum", [P, 1]), two("gr", [P, 1])
        ge = two("ge", [P, TOPK])
        oh = two("oh", [P, TOPK, E])
        ohs = two("ohs", [P, TOPK, E])
        msk, acc = two("msk", [P, E], BF16), two("acc", [P, E], BF16)
        pos = two("pos", [P, E])
        slf, sli = two("slf", [P, TOPK]), two("sli", [P, TOPK], I32)

        cnt, nbf, cum = sb("cnt", [P, E]), sb("nbf", [P, E]), sb("cum", [P, E])
        cnti, nbi = sb("cnti", [P, E], I32), sb("nbi", [P, E], I32)
        cmp_, cnb, eeq, cnn = (sb(n, [P, E]) for n in ("cmp_", "cnb", "eeq", "cnn"))
        ev, ib, nb_ = sb("ev", [P, 1]), sb("ib", [P, 1]), sb("nb_", [P, 1])
        ecl, lo_, t1, t2 = (sb(n, [P, 1]) for n in ("ecl", "lo_", "t1", "t2"))
        stt_ = sb("stt_", [P, 1])
        dg = sb("dg", [P, 4, NBP])
        tb = sb("tb", [P, 4, NBP])
        tbi = sb("tbi", [P, 2, NBP], I32)
        rowat = sb("rowat", [P, NBP])
        rp, g1, g2, pen = (sb(n, [P, NBP]) for n in ("rp", "g1", "g2", "pen"))

        RB = 4
        used[0] = 0
        xb = [view(ROW) for i in range(RB)]
        xbT = [view(P), view(P)]
        hb, hg, hT = ([view(F), view(F)] for n in range(3))
        sel4, sel4g = two("sel4", [P, TOPK]), two("sel4g", [P, TOPK])
        idf, idi, gt = two("idf", [P, 1]), [sb(f"idi{i}", [P, 1], I32) for i in range(RB)], two("gt", [P, 1])
        yb = [view(D), view(D)]
        yw = [view(D) for i in range(RB)]
        y4 = [view(TOPK, D) for i in range(4)]
        s4, r4, o4 = ([view(D), view(D)] for n in range(3))
        bn4, mv4, ve4, rv4 = two("bn4", [P, 6]), two("mv4", [P, 2]), two("ve4", [P, 1]), two("rv4", [P, 1])

        bank = [ctx.enter_context(nc.psum_tensor(f"bank{i}", [P, 512], F32)) for i in range(8)]

        xrows = nc.dram_tensor("xrows", (E * S, ROW), F32, kind="Internal").ap()
        yrows = nc.dram_tensor("yrows", (S * TOPK, D), F32, kind="Internal").ap()

        def c(name):
            return cst[:, at[name][0]:at[name][1]]

        def sm(name):
            return small[:, SMALL[name][0]:SMALL[name][1]]

        ident = c("ident")

        ld = {k: sem("ld_" + k) for k in "cst small dtlow xT win wout k x w1 w2 b1 b2".split()}
        zero_set, zero_out = sem("zero_set"), sem("zero_out")
        wc_mm, wc_cp, dtp_mm, s0v, s0a, dec_mm, gm_done, bf_done = (
            sem(n) for n in "wc_mm wc_cp dtp_mm s0v s0a dec_mm gm_done bf_done".split())
        ksq_done, ksq_mm, kb_done, wo_done0, clr = (sem(n) for n in "ksq_done ksq_mm kb_done wo_done0 clr".split())
        names = ("xt_cp pj_mm tr_mm sc0_mm sc1_mm st_mm y_mm yt_mm wo_mm x2t_mm lg_mm pos_mm "
                 "bc_dve sm0_dve sm1_dve y_add ms_dve yg_dve res_dve ve_dve x2_dve lg_dve oh_dve slot_dve gate_dve sil_dve "
                 "cb_act bd_act yt_act sq_act ez_act x2t_act x2c_act ge_act "
                 "pow1 pow2 c_st c_sil c_ln c_ra c_rb c_gate h_dve")
        s1 = {n: sem(n) for n in names.split()}
        sent = [sems(f"sent{k}", 2) for k in range(TOPK)]
        cnt_mm, c2, tb_mm, tab_done = (sem(n) for n in "cnt_mm c2 tb_mm tab_done".split())
        names3 = ("bt_mm h_mm ht_mm yb_mm bt_act hb_dve hg_act ht_act yb_dve yw_act c_id id_dve gt_dve")
        s3 = {n: sem(n) for n in names3.split()}
        got = sems("got", RB)
        put = sems("put", RB)
        names4 = "c_fin s_fin ve_fin pow_fin o_fin"
        sf = {n: sem(n) for n in names4.split()}
        y4in, oout = sems("y4in", 4), sems("oout", 2)

        block = ctx.enter_context(nc.Block())
        N1, N3 = NT + 6, NBP + 2
        LO1, LO3 = 6, 4

        @block.sync
        def _(sp):
            for k, dst, src in (("cst", cst, "consts"), ("dtlow", dtlow, "dtlow"), ("small", small, "small"),
                                ("xT", xT_all, "xT"), ("win", winT, "winT"), ("k", kT, "kT"),
                                ("wout", woutT, "woutT"), ("x", x_all, "x")):
                sp.dma_start(dst[:], d[src]).then_inc(ld[k], 16)
            sp.wait_ge(zero_set, 1)
            sp.dma_start(xrows.rearrange("(e r) w -> r e w", e=E)[0:P, :, :],
                         zrow[:].unsqueeze(1).broadcast_to([P, E, ROW])).then_inc(zero_out, 16)
            for k, dst, src in (("w1", w1s, "w1T"), ("w2", w2s, "w2T")):
                sp.dma_start(dst[:], d[src]).then_inc(ld[k], 16)
            sp.dma_start(b1s[:].rearrange("p e f -> p (e f)"), d["b1"].partition_broadcast(P)).then_inc(ld["b1"], 16)
            sp.dma_start(b2s[:].rearrange("p e f -> p (e f)"), d["b2"].partition_broadcast(P)).then_inc(ld["b2"], 16)

            sp.wait_ge(tab_done, 1)
            for k in range(TOPK):
                for j in range(2):
                    sp.wait_ge(sent[k][j], 16 * (NT // 2))

            def rows_in(s):
                b = s
                if not b.live(NBP):
                    return
                if b.had(RB):
                    sp.wait_ge(s3["bt_mm"], b.back(RB).count())
                    sp.wait_ge(s3["gt_dve"], b.back(RB).count())
                r = sp.value_load(tbi[0:1, 1, bass.ds(b.val(), 1)], min_val=0, max_val=E * S - P)
                sp.dma_start(xb[b.slot(RB)][:], xrows[bass.ds(r, P), :]).then_inc(got[b.slot(RB)], 16)

            run_steps(sp, rows_in, NBP, 4, LO3, NBP)

            for j in range(RB):
                sp.wait_ge(put[j], 16 * (NBP // RB))

            def tile_in(t):
                if t.had(4):
                    sp.wait_ge(sf["c_fin"], t.back(4).val(4, 1))
                sp.dma_start(y4[t.slot(4)][:].rearrange("p k d -> p (k d)"),
                             yrows.rearrange("(t k) d -> t (k d)", k=TOPK)[bass.ds(t.val(P), P), :]
                             ).then_inc(y4in[t.slot(4)], 16)

            run_steps(sp, tile_in, NT, 4, 4, NT)

        @block.tensor
        def _(pe):
            mm = pe.matmul
            pe.wait_ge(ld["dtlow"], 16)
            mm(bank[5][:, 0:H], dtlow[:, 0:D], dtlow[:, D:D + H], start=True, stop=True).then_inc(wc_mm, 1)
            pe.wait_ge(ld["xT"], 16)
            pe.wait_ge(wc_cp, 1)
            for t in range(NT):
                m = mm(bank[6][:, t * H:(t + 1) * H], xT_all[:, t * P:(t + 1) * P], wdt[:, :], start=True, stop=True)
            m.then_inc(dtp_mm, 1)
            pe.wait_ge(ksq_done, 1)
            pe.wait_ge(ld["cst"], 16)
            mm(bank[7][:, 0:E], c("ones"), ksq[:, :], start=True, stop=True).then_inc(ksq_mm, 1)
            pe.wait_ge(s0v, 5)
            mm(bank[3][:, 0:NT * H], c("decay"), dA[:, :], start=True, stop=True)
            mm(bank[4][:, 0:256], c("chunk0"), dA[:, :], start=True, stop=True)
            mm(bank[4][:, 256:512], c("chunk1"), dA[:, :], start=True, stop=True).then_inc(dec_mm, 1)

            def transposes(t):
                pe.wait_ge(s1["bc_dve"], t.count())
                if t.had(1):
                    pe.wait_ge(s1["bd_act"], t.back(1).count())
                b = t.slot(2)
                for j in range(2):
                    pe.transpose(bank[2][:, j * P:(j + 1) * P], cs[b][:, j * P:(j + 1) * P], ident)
                for j in range(2):
                    m = pe.transpose(bank[2][:, (2 + j) * P:(3 + j) * P], bs[b][:, j * P:(j + 1) * P], ident)
                m.then_inc(s1["tr_mm"], 1)

            def y_transpose(t):
                pe.wait_ge(s1["yg_dve"], t.count())
                if t.had(2):
                    pe.wait_ge(s1["x2t_act"], t.back(2).count())
                pe.transpose(bank[6][:, 0:P], yg[t.slot(2)][:, :], ident).then_inc(s1["yt_mm"], 1)

            def y_product(t):
                b = t.slot(2)
                pe.wait_ge(s1["h_dve"], t.val(NC, 1))
                pe.wait_ge(s1["cb_act"], t.count())
                if t.had(1):
                    pe.wait_ge(s1["y_add"], t.back(1).count())
                if t.had(4):
                    pe.wait_ge(s1["c_rb"], t.back(4).val(5, 2))
                for j in range(2):
                    for q in range(NC):
                        mm(bank[5][q * Q:(q + 1) * Q, j * 64:(j + 1) * 64], cb[b][:, j, q * Q:(q + 1) * Q],
                           hs[b][:, q, j, :], start=(j == 0), stop=False, skip_group_check=True)
                for h in range(H):
                    if h % HH == 0:
                        wait_apart(pe, [(s1[f"sm{h // HH}_dve"], t.count())], gm_done, 1)
                    for q in range(NC):
                        r = slice(q * Q, (q + 1) * Q)
                        m = mm(bank[5][r, h * HD:(h + 1) * HD], sc[b][r, h, :], xz[b][r, q, h * HD:(h + 1) * HD],
                               start=False, stop=(h == H - 1), skip_group_check=True)
                m.then_inc(s1["y_mm"], 1)

            def projection(t):
                b = t.slot(2)
                pe.wait_ge(s1["xt_cp"], t.count())
                if t.had(1):
                    pe.wait_ge(s1["bc_dve"], t.back(1).count())
                if t.had(4):
                    pe.wait_ge(s1["res_dve"], t.back(4).count())
                if t.had(5):
                    pe.wait_ge(s1["lg_dve"], t.back(5).count())
                mm(bank[0][:, :], xT[b][:, :], winT[:, 256:768], start=True, stop=True)
                mm(bank[1][:, 0:256], xT[b][:, :], winT[:, 0:256], start=True, stop=True).then_inc(s1["pj_mm"], 1)

            def states(t):
                b = t.slot(2)
                if t.had(1):
                    pe.wait_ge(s1["c_st"], t.val(NC))
                for j in range(2):
                    m = mm(bank[7][:, j * P:(j + 1) * P], bs[b][:, j * P:(j + 1) * P],
                           xz[b][:, :, j * 64:(j + 1) * 64], start=True, stop=True)
                m.then_inc(s1["st_mm"], 1)

            def out_product(t):
                pe.wait_ge(s1["yt_act"], t.count())
                pe.wait_ge(s1["bc_dve"], (t.back(-3) if not t.peeled or t.off + 3 < NT else Step(0, 2, NT - 1, True)).count())
                if t.had(1):
                    pe.wait_ge(s1["res_dve"], t.back(1).count())
                mm(bank[1][:, 256:384], yT[t.slot(2)][:, :], woutn[:, :], start=True, stop=True).then_inc(s1["wo_mm"], 1)

            def scores(t):
                b = t.slot(2)
                pe.wait_ge(s1["bd_act"], t.count())
                for j in range(2):
                    done = s1[f"sm{j}_dve"]
                    if t.had(1):
                        pe.wait_ge(done, t.back(1).count())
                    for q in range(NC):
                        m = mm(bank[3 + j][q * Q:(q + 1) * Q, :], cb[b][:, 2 + j, q * Q:(q + 1) * Q],
                               cbd[b][j][:, q, :, :].rearrange("p h i -> p (h i)"),
                               start=True, stop=True, skip_group_check=True)
                    m.then_inc(s1[f"sc{j}_mm"], 1)

            def x2_transpose(t):
                pe.wait_ge(s1["x2_dve"], t.count())
                if t.had(0):
                    nxt = t.back(-1)
                    if nxt.live(NT):
                        pe.wait_ge(s1["yt_act"], nxt.count())
                pe.transpose(bank[6][:, P:2 * P], x2[t.slot(2)][:, :], ident).then_inc(s1["x2t_mm"], 1)

            def router(t):
                pe.wait_ge(s1["x2t_act"], t.count())
                pe.wait_ge(s1["bc_dve"], (t.back(-4) if not t.peeled or t.off + 4 < NT else Step(0, 2, NT - 1, True)).count())
                if t.had(1):
                    pe.wait_ge(s1["lg_dve"], t.back(1).count())
                mm(bank[0][:, 0:E], x2T[t.slot(2)][:, :], kw[:, :], start=True, stop=True).then_inc(s1["lg_mm"], 1)

            def positions(t):
                b = t.slot(2)
                pe.wait_ge(s1["oh_dve"], t.count())
                if t.had(1):
                    pe.wait_ge(s1["c_rb"], t.back(1).val(5, 2))
                pe.wait_ge(s1["y_add"], (t.back(-3) if not t.peeled or t.off + 3 < NT else Step(0, 2, NT - 1, True)).count())
                mm(bank[5][:, 256:256 + E], before[:, :], msk[b][:, :], start=True, stop=False)
                mm(bank[5][:, 256:256 + E], ones16[:, :], acc[b][:, :], start=False, stop=True).then_inc(s1["pos_mm"], 1)

            def step(s):
                for fn, lag in ((transposes, 1), (y_transpose, 3), (y_product, 2), (projection, 0), (states, 1),
                                (out_product, 3), (scores, 1), (x2_transpose, 4), (router, 4), (positions, 5)):
                    if s.back(lag).live(NT):
                        fn(s.back(lag))

            pe.wait_ge(ld["win"], 16)
            pe.wait_ge(s0a, 6)
            pe.wait_ge(wo_done0, 1)
            pe.wait_ge(kb_done, 1)
            pe.wait_ge(gm_done, 1)
            run_steps(pe, step, NT, 2, LO1, N1)

            pe.wait_ge(s1["c_rb"], NT * 5)
            mm(bank[0][:, 0:E], ones16[:, :], acc[NT % 2][:, :], start=True, stop=True).then_inc(cnt_mm, 1)
            pe.wait_ge(c2, 18)
            mm(bank[0][:, 64:64 + 4 * NBP], c("ones"), dg[:].rearrange("p k b -> p (k b)"),
               start=True, stop=True).then_inc(tb_mm, 1)

            def rows_transpose(b):
                pe.wait_ge(got[b.slot(RB)], b.dma(RB))
                if b.had(1):
                    pe.wait_ge(s3["bt_act"], b.back(1).count())
                pe.transpose(bank[0][:, 0:P], xb[b.slot(RB)][:, 0:D], ident).then_inc(s3["bt_mm"], 1)

            def hidden(b):
                u = b.slot(2)
                ex = pe.value_load(tbi[0:1, 0, bass.ds(b.val(), 1)], min_val=0, max_val=E - 1)
                pe.wait_ge(s3["bt_act"], b.count())
                if b.had(2):
                    pe.wait_ge(s3["hb_dve"], b.back(2).count())
                mm(bank[1 + u][:, :], xbT[u][:, :], w1s[:, bass.ds(ex, 1), :], start=True, stop=True).then_inc(s3["h_mm"], 1)

            def hidden_transpose(b):
                u = b.slot(2)
                pe.wait_ge(s3["hg_act"], b.count())
                if b.had(2):
                    pe.wait_ge(s3["ht_act"], b.back(2).count())
                for f in range(FB):
                    m = pe.transpose(bank[3 + u][:, f * P:(f + 1) * P], hg[u][:, f * P:(f + 1) * P], ident)
                m.then_inc(s3["ht_mm"], 1)

            def expert_out(b):
                u = b.slot(2)
                ex = pe.value_load(tbi[0:1, 0, bass.ds(b.val(), 1)], min_val=0, max_val=E - 1)
                pe.wait_ge(s3["ht_act"], b.count())
                if b.had(2):
                    pe.wait_ge(s3["yb_dve"], b.back(2).count())
                for f in range(FB):
                    m = mm(bank[5 + u][:, 0:D], hT[u][:, f * P:(f + 1) * P], w2s[:, bass.ds(ex, 1), f, :],
                           start=(f == 0), stop=(f == FB - 1))
                m.then_inc(s3["yb_mm"], 1)

            def step3(s):
                for fn, lag in ((hidden, 0), (rows_transpose, -1), (hidden_transpose, 1), (expert_out, 2)):
                    if s.back(lag).live(NBP):
                        fn(s.back(lag))

            pe.wait_ge(tab_done, 1)
            pe.wait_ge(ld["w1"], 16)
            pe.wait_ge(ld["w2"], 16)
            rows_transpose(Step(0, 4, 0, True))
            run_steps(pe, step3, NBP - 4, 4, LO3, N3)

        @block.vector
        def _(ve):
            tt, ts_, stt = ve.tensor_tensor, ve.tensor_scalar, ve.scalar_tensor_tensor

            ve.memset(zrow[:], 0.0).then_inc(zero_set, 1)
            for i in range(2):
                ve.memset(xz[i][:], 0.0)
                ve.memset(acc[i][:], 0.0)
                ve.memset(hs[i][:], 0.0)
            ve.memset(gs[:, NT * NC - 1, :], 0.0).then_inc(clr, 1)
            ve.wait_ge(wc_mm, 1)
            ve.tensor_copy(wdt[:], bank[5][:, 0:H]).then_inc(wc_cp, 1)
            ve.wait_ge(ld["k"], 16)
            tt(ksq[:], kT[:, 0, :], kT[:, 0, :], ALU.mult).then_inc(ksq_done, 1)
            stt(out=kw[:], in0=kT[:, 0, :], scalar=2.0, in1=kT[:, 1, :], op0=ALU.mult, op1=ALU.add)
            ve.wait_ge(ld["cst"], 16)
            ve.tensor_copy(before[:], c("before"))
            ve.tensor_copy(ones16[:], c("ones")).then_inc(bf_done, 1)
            ve.wait_ge(ld["small"], 16)
            ve.wait_ge(dtp_mm, 1)

            def v3(a):
                return a[:].rearrange("p (t h) -> p t h", t=NT)

            def over_tiles(a):
                return a.unsqueeze(1).broadcast_to([P, NT, H])

            tt(v3(dtu), bank[6][:, 0:NT * H].rearrange("p (t h) -> p t h", t=NT), over_tiles(sm("dt_b")),
               ALU.add).then_inc(s0v, 1)
            ve.wait_ge(s0v, 1)
            stt(out=dta[:], in0=dtu[:], scalar=-1.0, in1=dtu[:], op0=ALU.mult, op1=ALU.min).then_inc(s0v, 1)
            ve.wait_ge(ksq_mm, 1)
            tt(kb[:], sm("rb"), bank[7][:, 0:E], ALU.subtract).then_inc(kb_done, 1)
            ve.wait_ge(ld["wout"], 16)
            ts_(woutn[:], woutT[:], sm("norm_w"), None, ALU.mult).then_inc(wo_done0, 1)
            ve.wait_ge(s0a, 3)
            stt(out=dts[:], in0=dtu[:], scalar=0.0, in1=dtl[:], op0=ALU.max, op1=ALU.add).then_inc(s0v, 1)
            ve.wait_ge(s0v, 3)
            stt(out=v3(dA), in0=v3(dts), scalar=-1.0, in1=over_tiles(expA[:]), op0=ALU.mult,
                op1=ALU.mult).then_inc(s0v, 2)
            ve.wait_ge(dec_mm, 1)
            for q in range(NC):
                m = ve.tensor_copy(ts[:, :, q, :], bank[4][:, q * 256:(q + 1) * 256].rearrange("p (t h) -> p t h", t=NT))
            m.then_inc(s0v, 1)
            ve.wait_ge(s0v, 6)
            ve.wait_ge(clr, 1)
            tsq = ts[:].rearrange("p t q h -> p (t q) h")
            tt(gs[:, 0:NT * NC - 1, :], tsq[:, 0:NT * NC - 1, :], tsq[:, 1:NT * NC, :], ALU.add).then_inc(s0v, 1)
            ve.wait_ge(s0a, 5)
            tt(fB[:].rearrange("p t h -> p (t h)"), dts[:], fE[:], ALU.mult)
            ve.wait_ge(s0a, 6)
            tt(gm[:], gx[:], c("head16").unsqueeze(1).broadcast_to([P, NT * NC, H]), ALU.mult).then_inc(gm_done, 1)
            ve.wait_ge(gm_done, 1)

            def y_add(t):
                b = t.slot(2)
                ve.wait_ge(s1["y_mm"], t.count())
                if t.had(2):
                    ve.wait_ge(s1["yg_dve"], t.back(2).count())
                    ve.wait_ge(s1["sq_act"], t.back(2).count())
                tt(yr[b][:], bank[5][:, 0:D], xd[b][:], ALU.add).then_inc(s1["y_add"], 1)

            def split(t):
                b = t.slot(2)
                ve.wait_ge(s1["pj_mm"], t.count())
                if t.had(2):
                    ve.wait_ge(s1["tr_mm"], t.back(2).count())
                    ve.wait_ge(s1["st_mm"], t.back(2).count())
                    ve.wait_ge(s1["y_mm"], t.back(2).count())
                    ve.wait_ge(s1["y_add"], t.back(2).count())
                    ve.wait_ge(s1["sil_dve"], t.back(2).count())
                    ve.wait_ge(s1["ez_act"], t.back(2).count())

                def hn(a):
                    return a.rearrange("p (h n) -> p h n", h=H)

                def f(a):
                    return a[:, bass.ds(t.val(), 1), :].rearrange("p o h -> p (o h)").unsqueeze(2).broadcast_to([P, H, NS])

                tt(hn(bs[b][:]), hn(bank[0][:, 0:256]), f(fB), ALU.mult)
                tt(hn(cs[b][:]), hn(bank[0][:, 256:512]), f(fC), ALU.mult)
                for q in range(NC):
                    r = slice(q * Q, (q + 1) * Q)
                    ve.tensor_copy(xz[b][r, q, :], bank[1][r, 0:D])
                tt(xd[b][:].rearrange("p (h w) -> p h w", h=H), bank[1][:, 0:D].rearrange("p (h w) -> p h w", h=H),
                   sm("D_param").unsqueeze(2).broadcast_to([P, H, HD]), ALU.mult)
                ve.tensor_copy(z[b][:], bank[1][:, D:2 * D]).then_inc(s1["bc_dve"], 1)

            def carry(t):
                b = t.slot(2)
                ve.wait_ge(s1["st_mm"], t.count())
                sv = bank[7][:, 0:2 * P].rearrange("p (j q w) -> p j q w", j=2, q=NC)
                for q in range(NC):
                    to = hs[b][:, 1, :, :] if q == 0 else hs[1 - b][:, 0, :, :]
                    if q == 0 and t.had(1):
                        ve.wait_ge(s1["h_dve"], t.val(NC))
                    if q == 1 and t.had(1):
                        ve.wait_ge(s1["y_mm"], t.back(1).count())
                    if q == 0 and t.had(2):
                        ve.wait_ge(s1["y_mm"], t.back(2).count())
                    if q == 1:
                        ve.wait_ge(s1["h_dve"], t.val(NC, 1))
                    tt(st[q][:], hs[b][:, q, :, :], sv[:, :, q, :], ALU.add).then_inc(s1["c_st"], 1)
                    ve.wait_ge(s1["c_st"], t.val(NC, q + 1))
                    g = gm[:, bass.ds(t.val(NC, q), 1), :].rearrange("p o h -> p (o h)").unsqueeze(2)
                    tt(to.rearrange("p j (h w) -> p (j h) w", h=HH), st[q][:].rearrange("p j (h w) -> p (j h) w", h=HH),
                       g.broadcast_to([P, H, HD]), ALU.mult).then_inc(s1["h_dve"], 1)

            def residual(t):
                b = t.slot(2)
                ve.wait_ge(s1["wo_mm"], t.count())
                if t.had(2):
                    ve.wait_ge(s1["x2_dve"], t.back(2).count())
                tt(res[b][:], bank[1][:, 256:384], x_all[:, bass.ds(t.val(), 1), :].rearrange("p o d -> p (o d)"),
                   ALU.add).then_inc(s1["res_dve"], 1)
                ve.wait_ge(s1["res_dve"], t.count())
                ve.bn_stats(bn[b][:], res[b][:]).then_inc(s1["c_ln"], 1)
                wait_apart(ve, [(s1["c_ln"], t.val(2, 1))], clr, 1)
                ve.bn_aggr(mv[b][:], bn[b][:]).then_inc(s1["c_ln"], 1)
                ve.wait_ge(s1["c_ln"], t.val(2, 2))
                if t.had(2):
                    ve.wait_ge(s1["pow2"], t.back(2).count())
                ts_(vre[b][:], mv[b][:, 1:2], EPS_LN, None, ALU.add).then_inc(s1["ve_dve"], 1)

            def causal(t, j):
                b = t.slot(2)
                ve.wait_ge(s1[f"sc{j}_mm"], t.count())
                if t.had(2):
                    ve.wait_ge(s1["y_mm"], t.back(2).count())
                tt(sc[b][:, j * HH:(j + 1) * HH, :], bank[3 + j][:, :].rearrange("p (h i) -> p h i", h=HH),
                   c("causal").unsqueeze(1).broadcast_to([P, HH, Q]), ALU.mult).then_inc(s1[f"sm{j}_dve"], 1)

            def mean_square(t):
                b = t.slot(2)
                ve.wait_ge(s1["sq_act"], t.count())
                if t.had(2):
                    ve.wait_ge(s1["pow1"], t.back(2).count())
                ts_(ms[b][:], ss[b][:], 1.0 / D, EPS_RMS, ALU.mult, ALU.add).then_inc(s1["ms_dve"], 1)

            def silu(t):
                b = t.slot(2)
                ve.wait_ge(s1["ez_act"], t.count())
                if t.had(2):
                    ve.wait_ge(s1["yg_dve"], t.back(2).count())
                ts_(ez1[b][:], ez[b][:], 1.0, None, ALU.add).then_inc(s1["c_sil"], 1)
                ve.wait_ge(s1["c_sil"], t.val(2, 1))
                ve.reciprocal(rz[b][:], ez1[b][:]).then_inc(s1["c_sil"], 1)
                ve.wait_ge(s1["c_sil"], t.val(2, 2))
                tt(sil[b][:], z[b][:], rz[b][:], ALU.mult).then_inc(s1["sil_dve"], 1)

            def gated(t):
                b = t.slot(2)
                ve.wait_ge(s1["pow1"], t.count())
                ve.wait_ge(s1["sil_dve"], t.count())
                if t.had(2):
                    ve.wait_ge(s1["yt_mm"], t.back(2).count())
                stt(out=yg[b][:], in0=yr[b][:], scalar=rs[b][:, 0:1], in1=sil[b][:], op0=ALU.mult,
                    op1=ALU.mult).then_inc(s1["yg_dve"], 1)

            def normed(t):
                b = t.slot(2)
                ve.wait_ge(s1["pow2"], t.count())
                if t.had(2):
                    ve.wait_ge(s1["x2t_mm"], t.back(2).count())
                    ve.wait_ge(s1["x2c_act"], t.back(2).count())
                ts_(x2[b][:], res[b][:], mv[b][:, 0:1], rv[b][:, 0:1], ALU.subtract,
                    ALU.mult).then_inc(s1["x2_dve"], 1)

            def route_a(t):
                b = t.slot(2)
                ve.wait_ge(s1["lg_mm"], t.count())
                ve.wait_ge(s1["x2c_act"], t.count())
                if t.had(2):
                    ve.wait_ge(s1["ge_act"], t.back(2).count())
                    ve.wait_ge(s1["pos_mm"], t.back(2).count())
                stt(out=lg[b][:], in0=bank[0][:, 0:E], scalar=xsq[b][:, 0:1], in1=kb[:], op0=ALU.subtract,
                    op1=ALU.add).then_inc(s1["lg_dve"], 1)
                wait_apart(ve, [(s1["lg_dve"], t.count())], clr, 1)
                ve.max(v8[b][:], lg[b][:]).then_inc(s1["c_ra"], 1)
                wait_apart(ve, [(s1["c_ra"], t.val(3, 1))], clr, 1)
                ve.max_index(i8[b][:], v8[b][:], lg[b][:]).then_inc(s1["c_ra"], 1)
                ts_(nv[b][:], v8[b][:, 0:1], -1.0, None, ALU.mult).then_inc(s1["gate_dve"], 1)
                ve.wait_ge(s1["c_ra"], t.val(3, 2))
                tt(oh[b][:], c("eids").rearrange("p (k e) -> p k e", k=TOPK),
                   i8[b][:, 0:TOPK].unsqueeze(2).broadcast_to([P, TOPK, E]), ALU.is_equal).then_inc(s1["c_ra"], 1)
                ve.wait_ge(s1["c_ra"], t.val(3, 3))
                with nc.allow_low_precision("0/1 values"):
                    ve.tensor_reduce(msk[b][:], oh[b][:].rearrange("p k e -> p e k"), AX_X, ALU.add).then_inc(s1["oh_dve"], 1)

            def route_b(t):
                b = t.slot(2)
                ve.wait_ge(s1["pos_mm"], t.count())
                if t.had(2):
                    for k in range(TOPK):
                        ve.wait_ge(sent[k][b], t.back(2).dma(2))
                ve.wait_ge(s1["oh_dve"], t.count())
                if t.had(1):
                    ve.wait_ge(s1["c_rb"], t.val(5))
                    ve.wait_ge(s1["pos_mm"], t.back(1).count())
                ve.tensor_copy(rows[b][:, 0:D], x2_all[:, bass.ds(t.val(), 1), :].rearrange("p o d -> p (o d)"))
                ve.tensor_copy(rows[b][:, RA:RI], i8[b][:, 0:TOPK])
                ve.tensor_copy(rows[b][:, RI:RG], c("tokid").rearrange("p (t k) -> p t k", t=NT)
                               [:, bass.ds(t.val(), 1), :].rearrange("p o k -> p (o k)"))
                tt(acc[1 - b][:], acc[b][:], msk[b][:], ALU.add).then_inc(s1["c_rb"], 1)
                tt(pos[b][:], bank[5][:, 256:256 + E], c("ebase"), ALU.add).then_inc(s1["c_rb"], 1)
                ve.wait_ge(s1["c_rb"], t.val(5, 2))
                tt(ohs[b][:], oh[b][:], pos[b][:].unsqueeze(1).broadcast_to([P, TOPK, E]), ALU.mult).then_inc(s1["c_rb"], 1)
                ve.wait_ge(s1["ge_act"], t.count())
                ve.reciprocal(gr[b][:], gsum[b][:]).then_inc(s1["c_gate"], 1)
                ve.wait_ge(s1["c_rb"], t.val(5, 3))
                ve.tensor_reduce(slf[b][:], ohs[b][:], AX_X, ALU.add).then_inc(s1["c_rb"], 1)
                ve.wait_ge(s1["c_gate"], t.count())
                ts_(rows[b][:, RG:ROW], ge[b][:], gr[b][:, 0:1], None, ALU.mult).then_inc(s1["c_rb"], 1)
                ve.wait_ge(s1["c_rb"], t.val(5, 4))
                ve.tensor_copy(sli[b][:], slf[b][:]).then_inc(s1["slot_dve"], 1)

            def step(s):
                for fn, lag in ((y_add, 2), (split, 0), (mean_square, 2), (carry, 1), (residual, 3),
                                (lambda t: causal(t, 0), 1), (silu, 1), (lambda t: causal(t, 1), 1), (gated, 2),
                                (normed, 3), (route_a, 4), (route_b, 5)):
                    if s.back(lag).live(NT):
                        fn(s.back(lag))

            ve.wait_ge(ld["x"], 16)
            ve.wait_ge(s0a, 6)
            run_steps(ve, step, NT, 2, LO1, N1)

            links = [0]

            def link(ins):
                links[0] += 1
                ins.then_inc(c2, 1)
                ve.wait_ge(c2, links[0])

            def floor128(dst, src):
                link(ts_(cnti[:], src, float(P - 1), None, ALU.add))
                link(ts_(nbi[:], cnti[:], 7, None, ALU.arith_shift_right))
                link(ve.tensor_copy(dst, nbi[:]))

            ve.wait_ge(cnt_mm, 1)
            link(ve.tensor_copy(cnt[:], bank[0][:, 0:E]))
            floor128(nbf[:], cnt[:])
            link(ve.tensor_tensor_scan(cum[:], c("ones")[:, 0:E], nbf[:], 0.0, ALU.mult, ALU.add))
            link(ts_(cmp_[:], cum[:], c("part"), None, ALU.is_le))
            link(ve.tensor_reduce(ev[:], cmp_[:], AX_X, ALU.add))
            link(tt(cnb[:], cmp_[:], nbf[:], ALU.mult))
            link(ve.tensor_reduce(ib[:], cnb[:], AX_X, ALU.add))
            link(ts_(eeq[:], c("eids")[:, 0:E], ev[:, 0:1], None, ALU.is_equal))
            link(tt(cnn[:], eeq[:], cnt[:], ALU.mult))
            link(ve.tensor_reduce(nb_[:], cnn[:], AX_X, ALU.add))
            link(ts_(ecl[:], ev[:], float(E - 1), None, ALU.min))
            link(stt(out=lo_[:], in0=ib[:], scalar=-float(P), in1=c("part128"), op0=ALU.mult, op1=ALU.add))
            link(stt(out=t1[:], in0=nb_[:], scalar=-float(P), in1=lo_[:], op0=ALU.add, op1=ALU.min))
            link(ts_(stt_[:], t1[:], 0.0, None, ALU.max))
            for k, v in enumerate((ecl, stt_, lo_, nb_)):
                m = ts_(dg[:, k, :], ident[:, 0:NBP], v[:, 0:1], None, ALU.mult)
            link(m)
            link(ts_(t2[:], t1[:], 0.0, None, ALU.max))
            ve.wait_ge(tb_mm, 1)
            link(ve.tensor_copy(tb[:].rearrange("p k b -> p (k b)"), bank[0][:, 64:64 + 4 * NBP]))
            link(stt(out=rowat[:], in0=tb[:, 0, :], scalar=float(S), in1=tb[:, 1, :], op0=ALU.mult, op1=ALU.add))
            link(ve.tensor_copy(tbi[:, 0, :], tb[:, 0, :]))
            ve.tensor_copy(tbi[:, 1, :], rowat[:]).then_inc(tab_done, 1)
            link(ts_(rp[:], tb[:, 1, :], c("part"), None, ALU.add))
            link(tt(g1[:], rp[:], tb[:, 2, :], ALU.is_ge))
            link(tt(g2[:], rp[:], tb[:, 3, :], ALU.is_lt))
            link(tt(rp[:], g1[:], g2[:], ALU.mult))
            link(ts_(pen[:], rp[:], -SKIP, SKIP, ALU.mult, ALU.add))

            def ids(b):
                u = b.slot(2)
                x = xb[b.slot(RB)]
                ve.wait_ge(got[b.slot(RB)], b.dma(RB))
                eid = tb[:, 0, bass.ds(b.val(), 1)]
                stt(out=sel4[u][:], in0=x[:, RA:RI], scalar=eid, in1=x[:, RI:RG], op0=ALU.is_equal, op1=ALU.mult)
                if b.had(2):
                    ve.wait_ge(s3["c_id"], b.back(2).val(2, 2))
                    ve.wait_ge(s3["yw_act"], b.back(2).count())
                stt(out=sel4g[u][:], in0=x[:, RA:RI], scalar=eid, in1=x[:, RG:ROW], op0=ALU.is_equal,
                    op1=ALU.mult).then_inc(s3["c_id"], 1)
                ve.wait_ge(s3["c_id"], b.val(2, 1))
                ve.tensor_reduce(idf[u][:], sel4[u][:], AX_X, ALU.add).then_inc(s3["c_id"], 1)
                ve.tensor_reduce(gt[u][:], sel4g[u][:], AX_X, ALU.add).then_inc(s3["gt_dve"], 1)
                ve.wait_ge(s3["c_id"], b.val(2, 2))
                if b.had(RB):
                    ve.wait_ge(put[b.slot(RB)], b.back(RB).dma(RB))
                tt(idi[b.slot(RB)][:], idf[u][:], pen[:, bass.ds(b.val(), 1)], ALU.add).then_inc(s3["id_dve"], 1)

            def hidden_bias(b):
                u = b.slot(2)
                ex = ve.value_load(tbi[0:1, 0, bass.ds(b.val(), 1)], min_val=0, max_val=E - 1)
                ve.wait_ge(s3["h_mm"], b.count())
                if b.had(2):
                    ve.wait_ge(s3["hg_act"], b.back(2).count())
                tt(hb[u][:], bank[1 + u][:, :], b1s[:, bass.ds(ex, 1), :].rearrange("p o f -> p (o f)"),
                   ALU.add).then_inc(s3["hb_dve"], 1)

            def out_bias(b):
                u = b.slot(2)
                ex = ve.value_load(tbi[0:1, 0, bass.ds(b.val(), 1)], min_val=0, max_val=E - 1)
                ve.wait_ge(s3["yb_mm"], b.count())
                if b.had(2):
                    ve.wait_ge(s3["yw_act"], b.back(2).count())
                tt(yb[u][:], bank[5 + u][:, 0:D], b2s[:, bass.ds(ex, 1), :].rearrange("p o f -> p (o f)"),
                   ALU.add).then_inc(s3["yb_dve"], 1)

            def step3(s):
                for fn, lag in ((hidden_bias, 0), (ids, 1), (out_bias, 2)):
                    if s.back(lag).live(NBP):
                        fn(s.back(lag))

            ve.wait_ge(ld["b1"], 16)
            ve.wait_ge(ld["b2"], 16)
            run_steps(ve, step3, NBP, 4, LO3, N3)

            def fin_sum(t):
                b = t.slot(2)
                ve.wait_ge(y4in[t.slot(4)], t.dma(4))
                ve.tensor_reduce(s4[b][:], y4[t.slot(4)][:].rearrange("p k d -> p d k"), AX_X, ALU.add).then_inc(sf["c_fin"], 1)
                ve.wait_ge(sf["c_fin"], t.val(4, 1))
                if t.had(2):
                    ve.wait_ge(sf["s_fin"], t.back(2).count())
                tt(r4[b][:], s4[b][:], x2_all[:, bass.ds(t.val(), 1), :].rearrange("p o d -> p (o d)"),
                   ALU.add).then_inc(sf["c_fin"], 1)
                ve.wait_ge(sf["c_fin"], t.val(4, 2))
                ve.bn_stats(bn4[b][:], r4[b][:]).then_inc(sf["c_fin"], 1)
                wait_apart(ve, [(sf["c_fin"], t.val(4, 3))], clr, 1)
                ve.bn_aggr(mv4[b][:], bn4[b][:]).then_inc(sf["c_fin"], 1)
                ve.wait_ge(sf["c_fin"], t.val(4, 4))
                ts_(ve4[b][:], mv4[b][:, 1:2], EPS_LN, None, ALU.add).then_inc(sf["ve_fin"], 1)

            def fin_norm(t):
                b = t.slot(2)
                ve.wait_ge(sf["pow_fin"], t.count())
                if t.had(2):
                    ve.wait_ge(oout[b], t.back(2).dma(2))
                ts_(o4[b][:], r4[b][:], mv4[b][:, 0:1], rv4[b][:, 0:1], ALU.subtract, ALU.mult).then_inc(sf["s_fin"], 1)

            def step4(s):
                for fn, lag in ((fin_sum, 0), (fin_norm, 1)):
                    if s.back(lag).live(NT):
                        fn(s.back(lag))

            run_steps(ve, step4, NT, 4, 4, NT + 1)

        @block.scalar
        def _(ac):
            act, cp = ac.activation, ACT.Copy

            ac.wait_ge(ld["small"], 16)
            act(expA[:], sm("A_log"), ACT.Exp).then_inc(s0a, 1)
            ac.wait_ge(s0v, 2)
            act(dte[:], dta[:], ACT.Exp).then_inc(s0a, 1)
            ac.wait_ge(s0a, 2)
            ac.wait_ge(ld["cst"], 16)
            act(dtl[:], dte[:], ACT.Ln, bias=c("ones")[:, 0:1]).then_inc(s0a, 1)
            ac.wait_ge(dec_mm, 1)
            act(fC[:].rearrange("p t h -> p (t h)"), bank[3][:, 0:256], ACT.Exp).then_inc(s0a, 1)
            act(fE[:], bank[3][:, 0:256], ACT.Exp, scale=-1.0).then_inc(s0a, 1)
            ac.wait_ge(s0v, 7)
            act(gx[:], gs[:], ACT.Exp, scale=0.5).then_inc(s0a, 1)

            def x_copy(t):
                if t.had(2):
                    ac.wait_ge(s1["pj_mm"], t.back(2).count())
                act(xT[t.slot(2)][:], xT_all[:, bass.ds(t.val(P), P)], cp).then_inc(s1["xt_cp"], 1)

            def block_diag(t):
                b = t.slot(2)
                ac.wait_ge(s1["tr_mm"], t.count())
                if t.had(2):
                    ac.wait_ge(s1["y_mm"], t.back(2).count())
                    ac.wait_ge(s1["sc1_mm"], t.back(2).count())
                act(cb[b][:].rearrange("p k t -> p (k t)"), bank[2][:, :], cp).then_inc(s1["cb_act"], 1)
                for j in range(2):
                    for h in range(HH):
                        m = act(cbd[b][j][:, :, h, :], bank[2][:, j * P:(j + 1) * P].rearrange("p (q i) -> p q i", q=NC),
                                cp, scale=c("head8")[:, h:h + 1])
                m.then_inc(s1["bd_act"], 1)

            def yT_copy(t):
                ac.wait_ge(s1["yt_mm"], t.count())
                if t.had(2):
                    ac.wait_ge(s1["wo_mm"], t.back(2).count())
                act(yT[t.slot(2)][:], bank[6][:, 0:P], cp).then_inc(s1["yt_act"], 1)

            def square(t):
                b = t.slot(2)
                ac.wait_ge(s1["y_add"], t.count())
                if t.had(2):
                    ac.wait_ge(s1["ms_dve"], t.back(2).count())
                act(ysq[b][:], yr[b][:], ACT.Square, accum_out=ss[b][:, 0:1]).then_inc(s1["sq_act"], 1)

            def exp_z(t):
                b = t.slot(2)
                ac.wait_ge(s1["bc_dve"], t.count())
                if t.had(2):
                    ac.wait_ge(s1["sil_dve"], t.back(2).count())
                act(ez[b][:], z[b][:], ACT.Exp, scale=-1.0).then_inc(s1["ez_act"], 1)

            def x2_copy(t):
                b = t.slot(2)
                ac.wait_ge(s1["x2t_mm"], t.count())
                if t.had(2):
                    ac.wait_ge(s1["lg_mm"], t.back(2).count())
                    ac.wait_ge(s1["lg_dve"], t.back(2).count())
                act(x2T[b][:], bank[6][:, P:2 * P], cp).then_inc(s1["x2t_act"], 1)
                act(x2sq[b][:], x2[b][:], ACT.Square, accum_out=xsq[b][:, 0:1])
                act(x2_all[:, bass.ds(t.val(), 1), :].rearrange("p o d -> p (o d)"), x2[b][:],
                    cp).then_inc(s1["x2c_act"], 1)

            def gate_exp(t):
                b = t.slot(2)
                ac.wait_ge(s1["gate_dve"], t.count())
                if t.had(2):
                    ac.wait_ge(s1["c_rb"], t.back(2).val(5, 5))
                act(ge[b][:], v8[b][:, 0:TOPK], ACT.Exp, bias=nv[b][:, 0:1], accum_out=gsum[b][:, 0:1]).then_inc(s1["ge_act"], 1)

            def step(s):
                for fn, lag in ((block_diag, 1), (yT_copy, 3), (square, 2), (exp_z, 0), (x_copy, -1),
                                (x2_copy, 4), (gate_exp, 4)):
                    if s.back(lag).live(NT):
                        fn(s.back(lag))

            ac.wait_ge(ld["xT"], 16)
            x_copy(Step(0, 2, 0, True))
            run_steps(ac, step, NT - 2, 2, LO1, N1)

            def bt_copy(b):
                ac.wait_ge(s3["bt_mm"], b.count())
                if b.had(2):
                    ac.wait_ge(s3["h_mm"], b.back(2).count())
                act(xbT[b.slot(2)][:], bank[0][:, 0:P], cp).then_inc(s3["bt_act"], 1)

            def gelu(b):
                u = b.slot(2)
                ac.wait_ge(s3["hb_dve"], b.count())
                if b.had(2):
                    ac.wait_ge(s3["ht_mm"], b.back(2).count())
                act(hg[u][:], hb[u][:], ACT.Gelu).then_inc(s3["hg_act"], 1)

            def ht_copy(b):
                u = b.slot(2)
                ac.wait_ge(s3["ht_mm"], b.count())
                if b.had(2):
                    ac.wait_ge(s3["yb_mm"], b.back(2).count())
                act(hT[u][:], bank[3 + u][:, :], cp).then_inc(s3["ht_act"], 1)

            def weigh(b):
                u, r = b.slot(2), b.slot(RB)
                ac.wait_ge(s3["yb_dve"], b.count())
                ac.wait_ge(s3["gt_dve"], b.count())
                if b.had(RB):
                    ac.wait_ge(put[r], b.back(RB).dma(RB))
                act(yw[r][:], yb[u][:], cp, scale=gt[u][:, 0:1]).then_inc(s3["yw_act"], 1)

            def step3(s):
                for fn, lag in ((bt_copy, -1), (gelu, 0), (ht_copy, 1), (weigh, 2)):
                    if s.back(lag).live(NBP):
                        fn(s.back(lag))

            bt_copy(Step(0, 4, 0, True))
            run_steps(ac, step3, NBP - 4, 4, LO3, N3)

            def store(t):
                b = t.slot(2)
                ac.wait_ge(sf["s_fin"], t.count())
                ac.dma_start(d["out"][bass.ds(t.val(P), P), :], o4[b][:]).then_inc(oout[b], 16)

            run_steps(ac, store, NT, 2, 2, NT)
            for j in range(2):
                ac.wait_ge(oout[j], 16 * (NT // 2))

        @block.gpsimd
        def _(po):
            po.wait_ge(ld["cst"], 16)
            mhalf = c("mhalf")

            def power(src, dst, ready, done, t):
                po.wait_ge(ready, t.count())
                po.tensor_tensor(dst[t.slot(2)][:], src[t.slot(2)][:], mhalf, ALU.pow).then_inc(done, 1)

            def pow_rms(t):
                if t.had(2):
                    po.wait_ge(s1["yg_dve"], t.back(2).count())
                power(ms, rs, s1["ms_dve"], s1["pow1"], t)

            def pow_ln(t):
                if t.had(2):
                    po.wait_ge(s1["x2_dve"], t.back(2).count())
                power(vre, rv, s1["ve_dve"], s1["pow2"], t)

            def send(t, ks):
                b = t.slot(2)
                wait_apart(po, [(s1["slot_dve"], t.count())], zero_out, 16)
                for k in ks:
                    po.indirect_dma_start(out=xrows, out_offset=bass.IndirectOffsetOnAxis(ap=sli[b][:, k:k + 1], axis=0),
                                          in_=rows[b][:, :], in_offset=None).then_inc(sent[k][b], 16)

            def step(s):
                for fn, lag in ((lambda t: send(t, (0, 1)), 6), (pow_rms, 2), (pow_ln, 3), (lambda t: send(t, (2, 3)), 6)):
                    if s.back(lag).live(NT):
                        fn(s.back(lag))

            po.wait_ge(zero_out, 16)
            run_steps(po, step, NT, 2, LO1, N1)

            def give(b):
                r = b.slot(RB)
                wait_apart(po, [(s3["yw_act"], b.count()), (s3["id_dve"], b.count())], zero_out, 16)
                po.indirect_dma_start(out=yrows, out_offset=bass.IndirectOffsetOnAxis(ap=idi[r][:, 0:1], axis=0),
                                      in_=yw[r][:, :], in_offset=None, bounds_check=S * TOPK - 1,
                                      oob_is_err=False).then_inc(put[r], 16)

            run_steps(po, give, NBP, 4, LO3, NBP)

            def pow_fin(t):
                if t.had(2):
                    po.wait_ge(sf["s_fin"], t.back(2).count())
                power(ve4, rv4, sf["ve_fin"], sf["pow_fin"], t)

            run_steps(po, pow_fin, NT, 2, 2, NT)


_OUT = ((1, 2048, 128), "float32")


def kernel(**inputs):
    import numpy as _np
    import concourse.bacc as _bacc
    from concourse import mybir as _mybir
    from concourse.bass_utils import run_bass_kernel_spmd as _run

    a = {k: _np.asarray(v) for k, v in inputs.items()}
    x = a["L0_attn_x"][0]
    win = a["L0_attn_W_in"]

    def rep(v):
        return _np.broadcast_to(v[None, :], (P, v.shape[0]))

    def flat(v):
        return _np.ascontiguousarray(v)

    host = {
        "consts": const_table()[1],
        "dtlow": flat(_np.concatenate([win[768:784], a["L0_attn_dt_W"].T], 1)),
        "small": flat(_np.concatenate([rep(a["L0_attn_dt_b"]), rep(a["L0_attn_A_log"]), rep(a["L0_attn_D_param"]),
                                       rep(a["L0_ffn_rb"]), a["L0_attn_norm_w"][:, None]], 1)),
        "xT": flat(x.T),
        "x": flat(x.reshape(NT, P, D).transpose(1, 0, 2)),
        "winT": flat(win[0:768].T),
        "woutT": flat(a["L0_attn_W_out"].T),
        "kT": flat(_np.stack([a["L0_ffn_keys"].T, a["L0_ffn_rw"].T], 1)),
        "w1T": flat(a["L0_ffn_w1"].transpose(2, 0, 1)),
        "w2T": flat(a["L0_ffn_w2"].transpose(2, 0, 1).reshape(FB, P, E, D).transpose(1, 2, 0, 3)),
        "b1": flat(a["L0_ffn_b1"].reshape(-1)),
        "b2": flat(a["L0_ffn_b2"].reshape(-1)),
    }
    nc = _bacc.Bacc("TRN2", target_bir_lowering=False, num_devices=1)
    d = {n: nc.dram_tensor(f"in_{n}", v.shape, _mybir.dt.from_np(v.dtype), kind="ExternalInput").ap() for n, v in host.items()}
    d["out"] = nc.dram_tensor("out_0", (S, D), F32, kind="ExternalOutput").ap()
    block_and_moe(nc, d)
    r = _run(nc, [{f"in_{n}": v for n, v in host.items()}], core_ids=[0])
    return r.results[0]["out_0"].reshape(_OUT[0])
```

```python
from contextlib import ExitStack

import numpy as np

import concourse.bass as bass
from concourse import mybir

ALU = mybir.AluOpType
ACT = mybir.ActivationFunctionType
AX_X = mybir.AxisListType.X
F32 = mybir.dt.float32
BF16 = mybir.dt.bfloat16
I32 = mybir.dt.int32
U32 = mybir.dt.uint32

P = 128
D = 128
S = 2048
NT = S // P
H, HD, NS = 16, 8, 16
Q = 64
NC = P // Q
HH = H // 2
E, TOPK, F = 16, 4, 512
FB = F // P
NBLK = S * TOPK // P + E - 1
NBP = NBLK + 1
ROW = D + 3 * TOPK
RA, RI, RG = D, D + TOPK, D + 2 * TOPK
SKIP = float(4 * S * TOPK)
EPS_LN, EPS_RMS = 1e-5, 1e-6


class Step:

    def __init__(self, base, unroll, off, peeled):
        self.base, self.unroll, self.off, self.peeled = base, unroll, off, peeled

    def back(self, k):
        return Step(self.base, self.unroll, self.off - k, self.peeled)

    def val(self, mul=1, add=0):
        fixed = self.off * mul + add
        return fixed if self.peeled else self.base * (self.unroll * mul) + fixed

    def count(self):
        return self.val(1, 1)

    def slot(self, ring):
        return self.off % ring

    def dma(self, ring):
        turn = self.off // ring
        return 16 * (turn + 1) if self.peeled else self.base * (16 * (self.unroll // ring)) + 16 * (turn + 1)

    def live(self, n):
        return not self.peeled or 0 <= self.off < n

    def had(self, k):
        return not self.peeled or self.off >= k


def run_steps(eng, body, n, unroll, lo, last, top=None):
    hi = lo + (n - lo) // unroll * unroll
    for s in range(lo):
        if top and s % unroll == 0:
            top(Step(0, unroll, s, True))
        body(Step(0, unroll, s, True))
    with eng.Fori(lo // unroll, hi // unroll) as i:
        if top:
            top(Step(i, unroll, 0, False))
        for u in range(unroll):
            body(Step(i, unroll, u, False))
    for s in range(hi, last):
        if top and s % unroll == 0:
            top(Step(0, unroll, s, True))
        body(Step(0, unroll, s, True))


def wait_apart(eng, waits, past, past_value):
    waits = [(sem, v if isinstance(v, int) else eng.to_reg(v)) for sem, v in waits]
    eng.wait_ge(past, past_value)
    for sem, v in waits:
        eng.wait_ge(sem, v)


def const_table():
    p = np.arange(P)[:, None]
    cols = {}
    cols["ident"] = np.eye(P)
    same = (p // Q) == (np.arange(P)[None] // Q)
    cols["decay"] = same * ((p <= np.arange(P)[None]) * 1.0 - 0.5)
    cols["chunk0"] = np.repeat((p < Q) * 1.0, P, 1)
    cols["chunk1"] = np.repeat((p >= Q) * 1.0, P, 1)
    cols["before"] = (p < np.arange(P)[None]) * 1.0
    cols["ones"] = np.ones((P, P))
    cols["causal"] = (p % Q <= np.arange(Q)[None]) * 1.0
    cols["head8"] = (p // NS == np.arange(HH)[None]) * 1.0
    cols["head16"] = (p // NS == np.arange(H)[None] % HH) * 1.0
    cols["eids"] = np.tile(np.arange(E), (P, TOPK)) * 1.0
    cols["ebase"] = np.tile(np.arange(E) * S, (P, 1)) * 1.0
    cols["tokid"] = (np.arange(NT)[None] * P + p)[:, :, None] * TOPK + np.arange(TOPK)[None, None] * 1.0
    cols["tokid"] = cols["tokid"].reshape(P, NT * TOPK)
    cols["part"] = p * 1.0
    cols["part128"] = p * 128.0
    cols["mhalf"] = np.full((P, 1), -0.5)
    at, out, n = {}, [], 0
    for k, v in cols.items():
        at[k] = (n, n + v.shape[1])
        n += v.shape[1]
        out.append(v.astype(np.float32))
    return at, np.ascontiguousarray(np.concatenate(out, 1))


SMALL = {"dt_b": (0, 16), "A_log": (16, 32), "D_param": (32, 48), "rb": (48, 64), "norm_w": (64, 65)}


def block_and_moe(nc, d, debug=None):
    at, _ = const_table()
    with ExitStack() as ctx:
        def sb(name, shape, dt=F32):
            return ctx.enter_context(nc.sbuf_tensor(name, shape, dt))

        def sem(name):
            return ctx.enter_context(nc.semaphore(name))

        def sems(name, n):
            return [sem(f"{name}{i}") for i in range(n)]

        cst = sb("cst", [P, at["mhalf"][1]])
        small = sb("small", [P, 65])
        dtlow = sb("dtlow", [16, D + 16])
        xT_all = sb("xT_all", [D, S])
        x_all = sb("x_all", [P, NT, D])
        winT = sb("winT", [D, 768])
        woutT = sb("woutT", [D, D])
        woutn = sb("woutn", [D, D])
        kT = sb("kT", [D, 2, E])
        kw = sb("kw", [D, E])
        ksq = sb("ksq", [D, E])
        kb = sb("kb", [P, E])
        w1s = sb("w1s", [D, E, F])
        w2s = sb("w2s", [P, E, FB, D])
        b1s = sb("b1s", [P, E, F])
        b2s = sb("b2s", [P, E, D])
        zrow = sb("zrow", [P, ROW])
        shared = sb("shared", [P, 8448])
        used = [0]

        def view(*shape):
            n = int(np.prod(shape))
            a = shared[:, used[0]:used[0] + n]
            used[0] += n
            if len(shape) > 1:
                names = " ".join("abcd"[:len(shape)])
                a = a.rearrange(f"p ({names}) -> p {names}", **dict(zip("abcd", shape)))
            return a

        wdt = sb("wdt", [D, H])
        dtu, dta, dte, dtl, dts, dA = (view(NT * H) for n in range(6))
        expA = sb("expA", [P, H])
        fC = sb("fC", [P, NT, H])
        fE = sb("fE", [P, NT * H])
        fB = sb("fB", [P, NT, H])
        ts, gs, gx = view(NT, NC, H), view(NT * NC, H), view(NT * NC, H)
        gm = sb("gm", [P, NT * NC, H])
        before = sb("before", [P, P], BF16)
        ones16 = sb("ones16", [P, P], BF16)

        def two(name, shape, dt=F32):
            return [sb(f"{name}{i}", shape, dt) for i in range(2)]

        used[0] = 0
        xT = two("xT", [D, P])
        cs, bs = two("cs", [P, H * NS]), two("bs", [P, H * NS])
        xz = two("xz", [P, NC, D])
        xd = two("xd", [P, D])
        z, ez, ez1, rz, sil = ([view(D), view(D)] for n in range(5))
        cb = [view(4, P), view(4, P)]
        cbd = [[view(NC, HH, Q) for j in range(2)] for i in range(2)]
        sc = [view(H, Q) for i in range(2)]
        st = two("st", [P, 2, D // 2])
        hs = two("hs", [P, NC, 2, D // 2])
        yr, ysq, yg, yT = (two(n, [P, D]) for n in ("yr", "ysq", "yg", "yT"))
        ss, ms, rs = (two(n, [P, 1]) for n in ("ss", "ms", "rs"))
        res = two("res", [P, D])
        bn = two("bn", [P, 6])
        mv, vre, rv = two("mv", [P, 2]), two("vre", [P, 1]), two("rv", [P, 1])
        rows = two("rows", [P, ROW])
        x2 = two("x2", [P, D])
        x2T, x2sq = two("x2T", [D, P]), two("x2sq", [P, D])
        xsq = two("xsq", [P, 1])
        x2_all = x_all
        lg = two("lg", [P, E])
        v8, i8 = two("v8", [P, 8]), two("i8", [P, 8], U32)
        nv, gsum, gr = two("nv", [P, 1]), two("gsum", [P, 1]), two("gr", [P, 1])
        ge = two("ge", [P, TOPK])
        oh = two("oh", [P, TOPK, E])
        ohs = two("ohs", [P, TOPK, E])
        msk, acc = two("msk", [P, E], BF16), two("acc", [P, E], BF16)
        pos = two("pos", [P, E])
        slf, sli = two("slf", [P, TOPK]), two("sli", [P, TOPK], I32)

        cnt, nbf, cum = sb("cnt", [P, E]), sb("nbf", [P, E]), sb("cum", [P, E])
        cnti, nbi = sb("cnti", [P, E], I32), sb("nbi", [P, E], I32)
        cmp_, cnb, eeq, cnn = (sb(n, [P, E]) for n in ("cmp_", "cnb", "eeq", "cnn"))
        ev, ib, nb_ = sb("ev", [P, 1]), sb("ib", [P, 1]), sb("nb_", [P, 1])
        ecl, lo_, t1, t2 = (sb(n, [P, 1]) for n in ("ecl", "lo_", "t1", "t2"))
        stt_ = sb("stt_", [P, 1])
        dg = sb("dg", [P, 4, NBP])
        tb = sb("tb", [P, 4, NBP])
        tbi = sb("tbi", [P, 2, NBP], I32)
        rowat = sb("rowat", [P, NBP])
        rp, g1, g2, pen = (sb(n, [P, NBP]) for n in ("rp", "g1", "g2", "pen"))

        RB = 4
        used[0] = 0
        xb = [view(ROW) for i in range(RB)]
        xbT = [view(P), view(P)]
        hb, hg, hT = ([view(F), view(F)] for n in range(3))
        sel4, sel4g = two("sel4", [P, TOPK]), two("sel4g", [P, TOPK])
        idf, gt = ([sb(f"{n}{i}", [P, 1]) for i in range(RB)] for n in ("idf", "gt"))
        idi = [sb(f"idi{i}", [P, 1], I32) for i in range(RB)]
        yb = [view(D), view(D)]
        yw = [view(D) for i in range(RB)]
        y4 = [view(TOPK, D) for i in range(4)]
        s4, r4, o4 = ([view(D), view(D)] for n in range(3))
        bn4, mv4, ve4, rv4 = two("bn4", [P, 6]), two("mv4", [P, 2]), two("ve4", [P, 1]), two("rv4", [P, 1])

        bank = [ctx.enter_context(nc.psum_tensor(f"bank{i}", [P, 512], F32)) for i in range(8)]

        xrows = nc.dram_tensor("xrows", (E * S, ROW), F32, kind="Internal").ap()
        yrows = nc.dram_tensor("yrows", (S * TOPK, D), F32, kind="Internal").ap()

        def c(name):
            return cst[:, at[name][0]:at[name][1]]

        def sm(name):
            return small[:, SMALL[name][0]:SMALL[name][1]]

        ident = c("ident")

        ld = {k: sem("ld_" + k) for k in "cst small dtlow xT win wout k x w1 w2 b1 b2".split()}
        zero_set, zero_out = sem("zero_set"), sem("zero_out")
        wc_mm, wc_cp, dtp_mm, s0v, s0a, dec_mm, gm_done, bf_done = (
            sem(n) for n in "wc_mm wc_cp dtp_mm s0v s0a dec_mm gm_done bf_done".split())
        ksq_done, ksq_mm, kb_done, wo_done0, clr = (sem(n) for n in "ksq_done ksq_mm kb_done wo_done0 clr".split())
        names = ("xt_cp bc_mm xz_mm tr_mm sc0_mm sc1_mm st_mm y_mm yt_mm wo_mm x2t_mm lg_mm pos_mm "
                 "bc_dve xz_dve sm0_dve sm1_dve y_add ms_dve yg_dve res_dve ve_dve x2_dve lg_dve oh_dve slot_dve gate_dve sil_dve "
                 "cb_act bd_act yt_act sq_act ez_act x2t_act x2c_act ge_act "
                 "pow1 pow2 c_st c_sil c_ln c_ra c_rb c_gate h_dve")
        s1 = {n: sem(n) for n in names.split()}
        sent = [sems(f"sent{k}", 2) for k in range(TOPK)]
        cnt_mm, c2, tb_mm, tab_done = (sem(n) for n in "cnt_mm c2 tb_mm tab_done".split())
        names3 = ("bt_mm h_mm ht_mm yb_mm bt_act hb_dve hg_act ht_act yb_dve yw_act c_id id_dve gt_dve")
        s3 = {n: sem(n) for n in names3.split()}
        got = sems("got", RB)
        put = sems("put", RB)
        names4 = "c_fin s_fin ve_fin pow_fin o_fin"
        sf = {n: sem(n) for n in names4.split()}
        y4in, oout = sems("y4in", 4), sems("oout", 2)

        block = ctx.enter_context(nc.Block())
        LAG3 = 3
        N1, N3 = NT + 6, NBP + LAG3
        LO1, LO3 = 6, 4

        def expert_registers(nc, table, engine):
            held = {}

            def load(first):
                lo = 0 if first.had(LAG3) else LAG3
                n = 4 + LAG3 - lo if not first.peeled else min(4 + LAG3, NBP - first.off + LAG3) - lo
                _, regs = nc.values_load_multi_w_load_instructions(
                    table[0:1, 0, bass.ds(first.back(LAG3 - lo).val(), n)], engines=[engine], min_val=0, max_val=E - 1,
                    skip_runtime_bounds_check_because="the table holds counts cut to E - 1")
                held.clear()
                held.update({first.off - LAG3 + lo + k: x for k, x in enumerate(regs)})

            return load, lambda b: held[b.off]

        @block.sync
        def _(sp):
            for k, dst, src in (("cst", cst, "consts"), ("dtlow", dtlow, "dtlow"), ("small", small, "small"),
                                ("xT", xT_all, "xT"), ("win", winT, "winT"), ("k", kT, "kT"),
                                ("wout", woutT, "woutT"), ("x", x_all, "x")):
                sp.dma_start(dst[:], d[src]).then_inc(ld[k], 16)
            sp.wait_ge(zero_set, 1)
            sp.dma_start(xrows.rearrange("(e r) w -> r e w", e=E)[0:P, :, :],
                         zrow[:].unsqueeze(1).broadcast_to([P, E, ROW])).then_inc(zero_out, 16)
            for k, dst, src in (("w1", w1s, "w1T"), ("w2", w2s, "w2T")):
                sp.dma_start(dst[:], d[src]).then_inc(ld[k], 16)
            sp.dma_start(b1s[:].rearrange("p e f -> p (e f)"), d["b1"].partition_broadcast(P)).then_inc(ld["b1"], 16)
            sp.dma_start(b2s[:].rearrange("p e f -> p (e f)"), d["b2"].partition_broadcast(P)).then_inc(ld["b2"], 16)

            sp.wait_ge(tab_done, 1)
            for k in range(TOPK):
                for j in range(2):
                    sp.wait_ge(sent[k][j], 16 * (NT // 2))

            def rows_in(s):
                b = s
                if not b.live(NBP):
                    return
                if b.had(RB):
                    sp.wait_ge(s3["bt_mm"], b.back(RB).count())
                    sp.wait_ge(s3["gt_dve"], b.back(RB).count())
                r = sp.value_load(tbi[0:1, 1, bass.ds(b.val(), 1)], min_val=0, max_val=E * S - P)
                sp.dma_start(xb[b.slot(RB)][:], xrows[bass.ds(r, P), :]).then_inc(got[b.slot(RB)], 16)

            run_steps(sp, rows_in, NBP, 4, LO3, NBP)

            for j in range(RB):
                sp.wait_ge(put[j], 16 * (NBP // RB))

            def tile_in(t):
                if t.had(4):
                    sp.wait_ge(sf["c_fin"], t.back(4).val(4, 1))
                sp.dma_start(y4[t.slot(4)][:].rearrange("p k d -> p (k d)"),
                             yrows.rearrange("(t k) d -> t (k d)", k=TOPK)[bass.ds(t.val(P), P), :]
                             ).then_inc(y4in[t.slot(4)], 16)

            run_steps(sp, tile_in, NT, 4, 4, NT)

        @block.tensor
        def _(pe):
            mm = pe.matmul
            pe.wait_ge(ld["dtlow"], 16)
            mm(bank[5][:, 0:H], dtlow[:, 0:D], dtlow[:, D:D + H], start=True, stop=True).then_inc(wc_mm, 1)
            pe.wait_ge(ld["xT"], 16)
            pe.wait_ge(wc_cp, 1)
            for t in range(NT):
                m = mm(bank[6][:, t * H:(t + 1) * H], xT_all[:, t * P:(t + 1) * P], wdt[:, :], start=True, stop=True)
            m.then_inc(dtp_mm, 1)
            pe.wait_ge(ksq_done, 1)
            pe.wait_ge(ld["cst"], 16)
            mm(bank[7][:, 0:E], c("ones"), ksq[:, :], start=True, stop=True).then_inc(ksq_mm, 1)
            pe.wait_ge(s0v, 5)
            mm(bank[3][:, 0:NT * H], c("decay"), dA[:, :], start=True, stop=True)
            mm(bank[4][:, 0:256], c("chunk0"), dA[:, :], start=True, stop=True)
            mm(bank[4][:, 256:512], c("chunk1"), dA[:, :], start=True, stop=True).then_inc(dec_mm, 1)

            def transposes(t):
                pe.wait_ge(s1["bc_dve"], t.count())
                if t.had(1):
                    pe.wait_ge(s1["bd_act"], t.back(1).count())
                b = t.slot(2)
                for j in range(2):
                    pe.transpose(bank[2][:, j * P:(j + 1) * P], cs[b][:, j * P:(j + 1) * P], ident)
                for j in range(2):
                    m = pe.transpose(bank[2][:, (2 + j) * P:(3 + j) * P], bs[b][:, j * P:(j + 1) * P], ident)
                m.then_inc(s1["tr_mm"], 1)

            def y_transpose(t):
                pe.wait_ge(s1["yg_dve"], t.count())
                if t.had(2):
                    pe.wait_ge(s1["x2t_act"], t.back(2).count())
                pe.transpose(bank[6][:, 0:P], yg[t.slot(2)][:, :], ident).then_inc(s1["yt_mm"], 1)

            def y_cross(t):
                b = t.slot(2)
                pe.wait_ge(s1["h_dve"], t.val(NC, 1))
                pe.wait_ge(s1["cb_act"], t.count())
                if t.had(1):
                    pe.wait_ge(s1["y_add"], t.back(1).count())
                for j in range(2):
                    for q in range(NC):
                        mm(bank[5][q * Q:(q + 1) * Q, j * 64:(j + 1) * 64], cb[b][:, j, q * Q:(q + 1) * Q],
                           hs[b][:, q, j, :], start=(j == 0), stop=False, skip_group_check=True)

            def y_intra(t, quarter):
                b = t.slot(2)
                for h in range(quarter * 4, quarter * 4 + 4):
                    if h % HH == 0:
                        wait_apart(pe, [(s1[f"sm{h // HH}_dve"], t.count())], gm_done, 1)
                    for q in range(NC):
                        r = slice(q * Q, (q + 1) * Q)
                        m = mm(bank[5][r, h * HD:(h + 1) * HD], sc[b][r, h, :], xz[b][r, q, h * HD:(h + 1) * HD],
                               start=False, stop=(h == H - 1), skip_group_check=True)
                if quarter == 3:
                    m.then_inc(s1["y_mm"], 1)

            def project_bc(t):
                pe.wait_ge(s1["xt_cp"], t.count())
                if t.had(1):
                    pe.wait_ge(s1["bc_dve"], t.back(1).count())
                mm(bank[0][:, :], xT[t.slot(2)][:, :], winT[:, 256:768], start=True, stop=True).then_inc(s1["bc_mm"], 1)

            def project_xz(t):
                if t.had(1):
                    pe.wait_ge(s1["xz_dve"], t.back(1).count())
                mm(bank[1][:, 0:256], xT[t.slot(2)][:, :], winT[:, 0:256], start=True, stop=True).then_inc(s1["xz_mm"], 1)

            def tail_read(s):
                for done, t, mul, add in ((s1["res_dve"], s.back(4), 1, 1), (s1["lg_dve"], s.back(5), 1, 1),
                                          (s1["c_rb"], s.back(6), 5, 2)):
                    if t.live(NT):
                        pe.wait_ge(done, t.val(mul, add))

            def states(t):
                b = t.slot(2)
                tail_read(t.back(-1))
                pe.wait_ge(s1["xz_dve"], t.count())
                if t.had(1):
                    pe.wait_ge(s1["c_st"], t.val(NC))
                for j in range(2):
                    m = mm(bank[7][:, j * P:(j + 1) * P], bs[b][:, j * P:(j + 1) * P],
                           xz[b][:, :, j * 64:(j + 1) * 64], start=True, stop=True)
                m.then_inc(s1["st_mm"], 1)

            def tail_free(s):
                if s.back(1).live(NT):
                    pe.wait_ge(s1["c_st"], s.back(1).val(NC, NC))
                else:
                    tail_read(s)

            def out_product(t):
                tail_free(t.back(-3))
                pe.wait_ge(s1["yt_act"], t.count())
                mm(bank[7][:, 256:384], yT[t.slot(2)][:, :], woutn[:, :], start=True, stop=True).then_inc(s1["wo_mm"], 1)

            def scores(t, j):
                if j == 0:
                    pe.wait_ge(s1["bd_act"], t.count())
                if t.had(1):
                    pe.wait_ge(s1[f"sm{j}_dve"], t.back(1).count())
                b = t.slot(2)
                for q in range(NC):
                    m = mm(bank[3 + j][q * Q:(q + 1) * Q, :], cb[b][:, 2 + j, q * Q:(q + 1) * Q],
                           cbd[b][j][:, q, :, :].rearrange("p h i -> p (h i)"),
                           start=True, stop=True, skip_group_check=True)
                m.then_inc(s1[f"sc{j}_mm"], 1)

            def x2_transpose(t):
                pe.wait_ge(s1["x2_dve"], t.count())
                if t.had(0):
                    nxt = t.back(-1)
                    if nxt.live(NT):
                        pe.wait_ge(s1["yt_act"], nxt.count())
                pe.transpose(bank[6][:, P:2 * P], x2[t.slot(2)][:, :], ident).then_inc(s1["x2t_mm"], 1)

            def router(t):
                if t.peeled and not t.back(-1).live(NT):
                    tail_free(t.back(-4))
                pe.wait_ge(s1["x2t_act"], t.count())
                mm(bank[7][:, 384:384 + E], x2T[t.slot(2)][:, :], kw[:, :], start=True, stop=True).then_inc(s1["lg_mm"], 1)

            def positions(t):
                b = t.slot(2)
                if t.peeled and not t.back(-1).live(NT):
                    tail_free(t.back(-5))
                pe.wait_ge(s1["oh_dve"], t.count())
                if t.had(1):
                    pe.wait_ge(s1["c_rb"], t.back(1).val(5, 2))
                mm(bank[7][:, 400:400 + E], before[:, :], msk[b][:, :], start=True, stop=False)
                mm(bank[7][:, 400:400 + E], ones16[:, :], acc[b][:, :], start=False, stop=True).then_inc(s1["pos_mm"], 1)

            def step(s):
                for fn, lag in ((transposes, 1), (y_cross, 2), (lambda t: y_intra(t, 0), 2), (project_bc, 0),
                                (lambda t: y_intra(t, 1), 2), (project_xz, 0), (lambda t: y_intra(t, 2), 2),
                                (states, 1), (y_transpose, 3), (lambda t: y_intra(t, 3), 2),
                                (lambda t: scores(t, 0), 1), (x2_transpose, 4), (lambda t: scores(t, 1), 1),
                                (out_product, 3), (router, 4), (positions, 5)):
                    if s.back(lag).live(NT):
                        fn(s.back(lag))

            pe.wait_ge(ld["win"], 16)
            pe.wait_ge(s0a, 6)
            pe.wait_ge(wo_done0, 1)
            pe.wait_ge(kb_done, 1)
            pe.wait_ge(gm_done, 1)
            run_steps(pe, step, NT, 2, LO1, N1)

            pe.wait_ge(s1["c_rb"], NT * 5)
            mm(bank[0][:, 0:E], ones16[:, :], acc[NT % 2][:, :], start=True, stop=True).then_inc(cnt_mm, 1)
            pe.wait_ge(c2, 18)
            mm(bank[0][:, 64:64 + 4 * NBP], c("ones"), dg[:].rearrange("p k b -> p (k b)"),
               start=True, stop=True).then_inc(tb_mm, 1)

            load_experts, expert = expert_registers(nc, tbi, mybir.EngineType.PE)

            def rows_transpose(b):
                pe.wait_ge(got[b.slot(RB)], b.dma(RB))
                if b.had(1):
                    pe.wait_ge(s3["bt_act"], b.back(1).count())
                pe.transpose(bank[0][:, 0:P], xb[b.slot(RB)][:, 0:D], ident).then_inc(s3["bt_mm"], 1)

            def hidden(b):
                u = b.slot(2)
                ex = expert(b)
                pe.wait_ge(s3["bt_act"], b.count())
                if b.had(2):
                    pe.wait_ge(s3["hb_dve"], b.back(2).count())
                mm(bank[1 + u][:, :], xbT[u][:, :], w1s[:, bass.ds(ex, 1), :], start=True, stop=True).then_inc(s3["h_mm"], 1)

            def hidden_transpose(b):
                u = b.slot(2)
                pe.wait_ge(s3["hg_act"], b.count())
                if b.had(2):
                    pe.wait_ge(s3["ht_act"], b.back(2).count())
                for f in range(FB):
                    m = pe.transpose(bank[3 + u][:, f * P:(f + 1) * P], hg[u][:, f * P:(f + 1) * P], ident)
                m.then_inc(s3["ht_mm"], 1)

            def expert_out(b):
                u = b.slot(2)
                ex = expert(b)
                pe.wait_ge(s3["ht_act"], b.count())
                if b.had(2):
                    pe.wait_ge(s3["yb_dve"], b.back(2).count())
                for f in range(FB):
                    m = mm(bank[5 + u][:, 0:D], hT[u][:, f * P:(f + 1) * P], w2s[:, bass.ds(ex, 1), f, :],
                           start=(f == 0), stop=(f == FB - 1))
                m.then_inc(s3["yb_mm"], 1)

            def step3(s):
                for fn, lag in ((expert_out, LAG3), (rows_transpose, -1), (hidden_transpose, 2), (hidden, 0)):
                    if s.back(lag).live(NBP):
                        fn(s.back(lag))

            pe.wait_ge(tab_done, 1)
            pe.wait_ge(ld["w1"], 16)
            pe.wait_ge(ld["w2"], 16)
            rows_transpose(Step(0, 4, 0, True))
            run_steps(pe, step3, NBP - 4, 4, LO3, N3, load_experts)

        @block.vector
        def _(ve):
            tt, ts_, stt = ve.tensor_tensor, ve.tensor_scalar, ve.scalar_tensor_tensor

            ve.memset(zrow[:], 0.0).then_inc(zero_set, 1)
            for i in range(2):
                ve.memset(xz[i][:], 0.0)
                ve.memset(acc[i][:], 0.0)
                ve.memset(hs[i][:], 0.0)
            ve.memset(gs[:, NT * NC - 1, :], 0.0).then_inc(clr, 1)
            ve.wait_ge(wc_mm, 1)
            ve.tensor_copy(wdt[:], bank[5][:, 0:H]).then_inc(wc_cp, 1)
            ve.wait_ge(ld["k"], 16)
            tt(ksq[:], kT[:, 0, :], kT[:, 0, :], ALU.mult).then_inc(ksq_done, 1)
            stt(out=kw[:], in0=kT[:, 0, :], scalar=2.0, in1=kT[:, 1, :], op0=ALU.mult, op1=ALU.add)
            ve.wait_ge(ld["cst"], 16)
            ve.tensor_copy(before[:], c("before"))
            ve.tensor_copy(ones16[:], c("ones")).then_inc(bf_done, 1)
            ve.wait_ge(ld["small"], 16)
            ve.wait_ge(dtp_mm, 1)

            def v3(a):
                return a[:].rearrange("p (t h) -> p t h", t=NT)

            def over_tiles(a):
                return a.unsqueeze(1).broadcast_to([P, NT, H])

            tt(v3(dtu), bank[6][:, 0:NT * H].rearrange("p (t h) -> p t h", t=NT), over_tiles(sm("dt_b")),
               ALU.add).then_inc(s0v, 1)
            ve.wait_ge(s0v, 1)
            stt(out=dta[:], in0=dtu[:], scalar=-1.0, in1=dtu[:], op0=ALU.mult, op1=ALU.min).then_inc(s0v, 1)
            ve.wait_ge(ksq_mm, 1)
            tt(kb[:], sm("rb"), bank[7][:, 0:E], ALU.subtract).then_inc(kb_done, 1)
            ve.wait_ge(ld["wout"], 16)
            ts_(woutn[:], woutT[:], sm("norm_w"), None, ALU.mult).then_inc(wo_done0, 1)
            ve.wait_ge(s0a, 3)
            stt(out=dts[:], in0=dtu[:], scalar=0.0, in1=dtl[:], op0=ALU.max, op1=ALU.add).then_inc(s0v, 1)
            ve.wait_ge(s0v, 3)
            stt(out=v3(dA), in0=v3(dts), scalar=-1.0, in1=over_tiles(expA[:]), op0=ALU.mult,
                op1=ALU.mult).then_inc(s0v, 2)
            ve.wait_ge(dec_mm, 1)
            for q in range(NC):
                m = ve.tensor_copy(ts[:, :, q, :], bank[4][:, q * 256:(q + 1) * 256].rearrange("p (t h) -> p t h", t=NT))
            m.then_inc(s0v, 1)
            ve.wait_ge(s0v, 6)
            ve.wait_ge(clr, 1)
            tsq = ts[:].rearrange("p t q h -> p (t q) h")
            tt(gs[:, 0:NT * NC - 1, :], tsq[:, 0:NT * NC - 1, :], tsq[:, 1:NT * NC, :], ALU.add).then_inc(s0v, 1)
            ve.wait_ge(s0a, 5)
            tt(fB[:].rearrange("p t h -> p (t h)"), dts[:], fE[:], ALU.mult)
            ve.wait_ge(s0a, 6)
            tt(gm[:], gx[:], c("head16").unsqueeze(1).broadcast_to([P, NT * NC, H]), ALU.mult).then_inc(gm_done, 1)
            ve.wait_ge(gm_done, 1)

            def y_add(t):
                b = t.slot(2)
                ve.wait_ge(s1["y_mm"], t.count())
                if t.had(2):
                    ve.wait_ge(s1["yg_dve"], t.back(2).count())
                    ve.wait_ge(s1["sq_act"], t.back(2).count())
                tt(yr[b][:], bank[5][:, 0:D], xd[b][:], ALU.add).then_inc(s1["y_add"], 1)

            def scale_bc(t):
                b = t.slot(2)
                ve.wait_ge(s1["bc_mm"], t.count())
                if t.had(2):
                    ve.wait_ge(s1["tr_mm"], t.back(2).count())
                    ve.wait_ge(s1["st_mm"], t.back(2).count())

                def hn(a):
                    return a.rearrange("p (h n) -> p h n", h=H)

                def f(a):
                    return a[:, bass.ds(t.val(), 1), :].rearrange("p o h -> p (o h)").unsqueeze(2).broadcast_to([P, H, NS])

                tt(hn(bs[b][:]), hn(bank[0][:, 0:256]), f(fB), ALU.mult)
                tt(hn(cs[b][:]), hn(bank[0][:, 256:512]), f(fC), ALU.mult).then_inc(s1["bc_dve"], 1)

            def take_x(t):
                b = t.slot(2)
                ve.wait_ge(s1["xz_mm"], t.count())
                if t.had(2):
                    ve.wait_ge(s1["y_mm"], t.back(2).count())
                for q in range(NC):
                    r = slice(q * Q, (q + 1) * Q)
                    ve.tensor_copy(xz[b][r, q, :], bank[1][r, 0:D])

            def take_dx(t):
                b = t.slot(2)
                if t.had(2):
                    ve.wait_ge(s1["y_add"], t.back(2).count())
                tt(xd[b][:].rearrange("p (h w) -> p h w", h=H), bank[1][:, 0:D].rearrange("p (h w) -> p h w", h=H),
                   sm("D_param").unsqueeze(2).broadcast_to([P, H, HD]), ALU.mult)

            def take_z(t):
                b = t.slot(2)
                if t.had(2):
                    ve.wait_ge(s1["sil_dve"], t.back(2).count())
                    ve.wait_ge(s1["ez_act"], t.back(2).count())
                ve.tensor_copy(z[b][:], bank[1][:, D:2 * D]).then_inc(s1["xz_dve"], 1)

            def states_after(t, q):
                return hs[t.slot(2)][:, 1, :, :] if q == 0 else hs[1 - t.slot(2)][:, 0, :, :]

            def carry_sum(t, q):
                b = t.slot(2)
                sv = bank[7][:, 0:2 * P].rearrange("p (j q w) -> p j q w", j=2, q=NC)
                if q == 0:
                    ve.wait_ge(s1["st_mm"], t.count())
                if q == 1 or t.had(1):
                    ve.wait_ge(s1["h_dve"], t.val(NC, q))
                tt(st[q][:], hs[b][:, q, :, :], sv[:, :, q, :], ALU.add).then_inc(s1["c_st"], 1)

            def carry_scale(t, q):
                if q == 1 and t.had(1):
                    ve.wait_ge(s1["y_mm"], t.back(1).count())
                if q == 0 and t.had(2):
                    ve.wait_ge(s1["y_mm"], t.back(2).count())
                ve.wait_ge(s1["c_st"], t.val(NC, q + 1))
                g = gm[:, bass.ds(t.val(NC, q), 1), :].rearrange("p o h -> p (o h)").unsqueeze(2)
                tt(states_after(t, q).rearrange("p j (h w) -> p (j h) w", h=HH),
                   st[q][:].rearrange("p j (h w) -> p (j h) w", h=HH),
                   g.broadcast_to([P, H, HD]), ALU.mult).then_inc(s1["h_dve"], 1)

            def residual(t):
                b = t.slot(2)
                for done, lag in ((s1["pos_mm"], 2), (s1["lg_mm"], 1), (s1["wo_mm"], 0)):
                    if t.back(lag).live(NT):
                        ve.wait_ge(done, t.back(lag).count())
                        break
                if t.had(2):
                    ve.wait_ge(s1["x2_dve"], t.back(2).count())
                tt(res[b][:], bank[7][:, 256:384], x_all[:, bass.ds(t.val(), 1), :].rearrange("p o d -> p (o d)"),
                   ALU.add).then_inc(s1["res_dve"], 1)

            def res_stats(t):
                ve.wait_ge(s1["res_dve"], t.count())
                ve.bn_stats(bn[t.slot(2)][:], res[t.slot(2)][:]).then_inc(s1["c_ln"], 1)

            def res_moments(t):
                wait_apart(ve, [(s1["c_ln"], t.val(2, 1))], clr, 1)
                ve.bn_aggr(mv[t.slot(2)][:], bn[t.slot(2)][:]).then_inc(s1["c_ln"], 1)

            def res_var(t):
                ve.wait_ge(s1["c_ln"], t.val(2, 2))
                if t.had(2):
                    ve.wait_ge(s1["pow2"], t.back(2).count())
                ts_(vre[t.slot(2)][:], mv[t.slot(2)][:, 1:2], EPS_LN, None, ALU.add).then_inc(s1["ve_dve"], 1)

            def causal(t, j):
                b = t.slot(2)
                ve.wait_ge(s1[f"sc{j}_mm"], t.count())
                if t.had(2):
                    ve.wait_ge(s1["y_mm"], t.back(2).count())
                tt(sc[b][:, j * HH:(j + 1) * HH, :], bank[3 + j][:, :].rearrange("p (h i) -> p h i", h=HH),
                   c("causal").unsqueeze(1).broadcast_to([P, HH, Q]), ALU.mult).then_inc(s1[f"sm{j}_dve"], 1)

            def mean_square(t):
                b = t.slot(2)
                ve.wait_ge(s1["sq_act"], t.count())
                if t.had(2):
                    ve.wait_ge(s1["pow1"], t.back(2).count())
                ts_(ms[b][:], ss[b][:], 1.0 / D, EPS_RMS, ALU.mult, ALU.add).then_inc(s1["ms_dve"], 1)

            def silu_den(t):
                b = t.slot(2)
                ve.wait_ge(s1["ez_act"], t.count())
                ts_(ez1[b][:], ez[b][:], 1.0, None, ALU.add).then_inc(s1["c_sil"], 1)

            def silu_inv(t):
                ve.wait_ge(s1["c_sil"], t.val(2, 1))
                ve.reciprocal(rz[t.slot(2)][:], ez1[t.slot(2)][:]).then_inc(s1["c_sil"], 1)

            def silu_out(t):
                b = t.slot(2)
                ve.wait_ge(s1["c_sil"], t.val(2, 2))
                if t.had(2):
                    ve.wait_ge(s1["yg_dve"], t.back(2).count())
                tt(sil[b][:], z[b][:], rz[b][:], ALU.mult).then_inc(s1["sil_dve"], 1)

            def gated(t):
                b = t.slot(2)
                ve.wait_ge(s1["pow1"], t.count())
                ve.wait_ge(s1["sil_dve"], t.count())
                if t.had(2):
                    ve.wait_ge(s1["yt_mm"], t.back(2).count())
                stt(out=yg[b][:], in0=yr[b][:], scalar=rs[b][:, 0:1], in1=sil[b][:], op0=ALU.mult,
                    op1=ALU.mult).then_inc(s1["yg_dve"], 1)

            def normed(t):
                b = t.slot(2)
                ve.wait_ge(s1["pow2"], t.count())
                if t.had(2):
                    ve.wait_ge(s1["x2t_mm"], t.back(2).count())
                    ve.wait_ge(s1["x2c_act"], t.back(2).count())
                ts_(x2[b][:], res[b][:], mv[b][:, 0:1], rv[b][:, 0:1], ALU.subtract,
                    ALU.mult).then_inc(s1["x2_dve"], 1)

            def logits(t):
                b = t.slot(2)
                for done, lag in ((s1["pos_mm"], 1), (s1["lg_mm"], 0)):
                    if t.back(lag).live(NT):
                        ve.wait_ge(done, t.back(lag).count())
                        break
                ve.wait_ge(s1["x2c_act"], t.count())
                stt(out=lg[b][:], in0=bank[7][:, 384:384 + E], scalar=xsq[b][:, 0:1], in1=kb[:], op0=ALU.subtract,
                    op1=ALU.add).then_inc(s1["lg_dve"], 1)

            def best(t):
                b = t.slot(2)
                used = [(s1["ge_act"], t.back(2).count())] if t.had(2) else []
                wait_apart(ve, used + [(s1["lg_dve"], t.count())], clr, 1)
                ve.max(v8[b][:], lg[b][:]).then_inc(s1["c_ra"], 1)

            def best_ids(t):
                b = t.slot(2)
                wait_apart(ve, [(s1["c_ra"], t.val(3, 1))], clr, 1)
                ve.max_index(i8[b][:], v8[b][:], lg[b][:]).then_inc(s1["c_ra"], 1)
                ts_(nv[b][:], v8[b][:, 0:1], -1.0, None, ALU.mult).then_inc(s1["gate_dve"], 1)

            def one_hot(t):
                b = t.slot(2)
                ve.wait_ge(s1["c_ra"], t.val(3, 2))
                tt(oh[b][:], c("eids").rearrange("p (k e) -> p k e", k=TOPK),
                   i8[b][:, 0:TOPK].unsqueeze(2).broadcast_to([P, TOPK, E]), ALU.is_equal).then_inc(s1["c_ra"], 1)

            def chosen(t):
                b = t.slot(2)
                ve.wait_ge(s1["c_ra"], t.val(3, 3))
                if t.had(2):
                    ve.wait_ge(s1["pos_mm"], t.back(2).count())
                with nc.allow_low_precision("0/1 values"):
                    ve.tensor_reduce(msk[b][:], oh[b][:].rearrange("p k e -> p e k"), AX_X, ALU.add).then_inc(s1["oh_dve"], 1)

            def pack_row(t):
                b = t.slot(2)
                if t.had(2):
                    for k in range(TOPK):
                        ve.wait_ge(sent[k][b], t.back(2).dma(2))
                ve.tensor_copy(rows[b][:, 0:D], x2_all[:, bass.ds(t.val(), 1), :].rearrange("p o d -> p (o d)"))
                ve.wait_ge(s1["oh_dve"], t.count())
                ve.tensor_copy(rows[b][:, RA:RI], i8[b][:, 0:TOPK])
                ve.tensor_copy(rows[b][:, RI:RG], c("tokid").rearrange("p (t k) -> p t k", t=NT)
                               [:, bass.ds(t.val(), 1), :].rearrange("p o k -> p (o k)"))

            def place(t):
                b = t.slot(2)
                ve.wait_ge(s1["pos_mm"], t.count())
                if t.had(1):
                    ve.wait_ge(s1["c_rb"], t.val(5))
                tt(acc[1 - b][:], acc[b][:], msk[b][:], ALU.add).then_inc(s1["c_rb"], 1)
                tt(pos[b][:], bank[7][:, 400:400 + E], c("ebase"), ALU.add).then_inc(s1["c_rb"], 1)

            def place_of_chosen(t):
                b = t.slot(2)
                ve.wait_ge(s1["c_rb"], t.val(5, 2))
                tt(ohs[b][:], oh[b][:], pos[b][:].unsqueeze(1).broadcast_to([P, TOPK, E]), ALU.mult).then_inc(s1["c_rb"], 1)

            def gate_inv(t):
                ve.wait_ge(s1["ge_act"], t.count())
                ve.reciprocal(gr[t.slot(2)][:], gsum[t.slot(2)][:]).then_inc(s1["c_gate"], 1)

            def slots(t):
                ve.wait_ge(s1["c_rb"], t.val(5, 3))
                ve.tensor_reduce(slf[t.slot(2)][:], ohs[t.slot(2)][:], AX_X, ALU.add).then_inc(s1["c_rb"], 1)

            def gates(t):
                b = t.slot(2)
                ve.wait_ge(s1["c_gate"], t.count())
                ts_(rows[b][:, RG:ROW], ge[b][:], gr[b][:, 0:1], None, ALU.mult).then_inc(s1["c_rb"], 1)

            def slots_out(t):
                ve.wait_ge(s1["c_rb"], t.val(5, 4))
                ve.tensor_copy(sli[t.slot(2)][:], slf[t.slot(2)][:]).then_inc(s1["slot_dve"], 1)

            def step(s):
                for fn, lag in ((scale_bc, 0), (y_add, 2), (take_x, 0), (lambda t: carry_sum(t, 0), 1), (take_dx, 0),
                                (lambda t: carry_scale(t, 0), 1), (take_z, 0), (lambda t: carry_sum(t, 1), 1),
                                (silu_den, 1), (lambda t: carry_scale(t, 1), 1), (silu_inv, 1), (mean_square, 2),
                                (silu_out, 1), (lambda t: causal(t, 0), 1), (gated, 2), (lambda t: causal(t, 1), 1),
                                (residual, 3), (logits, 4), (pack_row, 5), (res_stats, 3), (best, 4), (place, 5),
                                (res_moments, 3), (best_ids, 4), (place_of_chosen, 5), (res_var, 3),
                                (one_hot, 4), (gate_inv, 5), (slots, 5), (chosen, 4), (gates, 5), (slots_out, 5),
                                (normed, 3)):
                    if s.back(lag).live(NT):
                        fn(s.back(lag))

            ve.wait_ge(ld["x"], 16)
            ve.wait_ge(s0a, 6)
            run_steps(ve, step, NT, 2, LO1, N1)

            links = [0]

            def link(ins):
                links[0] += 1
                ins.then_inc(c2, 1)
                ve.wait_ge(c2, links[0])

            def floor128(dst, src):
                link(ts_(cnti[:], src, float(P - 1), None, ALU.add))
                link(ts_(nbi[:], cnti[:], 7, None, ALU.arith_shift_right))
                link(ve.tensor_copy(dst, nbi[:]))

            ve.wait_ge(cnt_mm, 1)
            link(ve.tensor_copy(cnt[:], bank[0][:, 0:E]))
            floor128(nbf[:], cnt[:])
            link(ve.tensor_tensor_scan(cum[:], c("ones")[:, 0:E], nbf[:], 0.0, ALU.mult, ALU.add))
            link(ts_(cmp_[:], cum[:], c("part"), None, ALU.is_le))
            link(ve.tensor_reduce(ev[:], cmp_[:], AX_X, ALU.add))
            link(tt(cnb[:], cmp_[:], nbf[:], ALU.mult))
            link(ve.tensor_reduce(ib[:], cnb[:], AX_X, ALU.add))
            link(ts_(eeq[:], c("eids")[:, 0:E], ev[:, 0:1], None, ALU.is_equal))
            link(tt(cnn[:], eeq[:], cnt[:], ALU.mult))
            link(ve.tensor_reduce(nb_[:], cnn[:], AX_X, ALU.add))
            link(ts_(ecl[:], ev[:], float(E - 1), None, ALU.min))
            link(stt(out=lo_[:], in0=ib[:], scalar=-float(P), in1=c("part128"), op0=ALU.mult, op1=ALU.add))
            link(stt(out=t1[:], in0=nb_[:], scalar=-float(P), in1=lo_[:], op0=ALU.add, op1=ALU.min))
            link(ts_(stt_[:], t1[:], 0.0, None, ALU.max))
            for k, v in enumerate((ecl, stt_, lo_, nb_)):
                m = ts_(dg[:, k, :], ident[:, 0:NBP], v[:, 0:1], None, ALU.mult)
            link(m)
            link(ts_(t2[:], t1[:], 0.0, None, ALU.max))
            ve.wait_ge(tb_mm, 1)
            link(ve.tensor_copy(tb[:].rearrange("p k b -> p (k b)"), bank[0][:, 64:64 + 4 * NBP]))
            link(stt(out=rowat[:], in0=tb[:, 0, :], scalar=float(S), in1=tb[:, 1, :], op0=ALU.mult, op1=ALU.add))
            link(ve.tensor_copy(tbi[:, 0, :], tb[:, 0, :]))
            ve.tensor_copy(tbi[:, 1, :], rowat[:]).then_inc(tab_done, 1)
            link(ts_(rp[:], tb[:, 1, :], c("part"), None, ALU.add))
            link(tt(g1[:], rp[:], tb[:, 2, :], ALU.is_ge))
            link(tt(g2[:], rp[:], tb[:, 3, :], ALU.is_lt))
            link(tt(rp[:], g1[:], g2[:], ALU.mult))
            link(ts_(pen[:], rp[:], -SKIP, SKIP, ALU.mult, ALU.add))

            load_experts, expert = expert_registers(nc, tbi, mybir.EngineType.DVE)

            def ids(b):
                u, r = b.slot(2), b.slot(RB)
                x = xb[r]
                ve.wait_ge(got[r], b.dma(RB))
                if b.had(2):
                    ve.wait_ge(s3["gt_dve"], b.back(2).count())
                eid = tb[:, 0, bass.ds(b.val(), 1)]
                stt(out=sel4[u][:], in0=x[:, RA:RI], scalar=eid, in1=x[:, RI:RG], op0=ALU.is_equal, op1=ALU.mult)
                stt(out=sel4g[u][:], in0=x[:, RA:RI], scalar=eid, in1=x[:, RG:ROW], op0=ALU.is_equal,
                    op1=ALU.mult).then_inc(s3["c_id"], 1)
                ve.wait_ge(s3["c_id"], b.count())
                if b.had(RB):
                    ve.wait_ge(s3["id_dve"], b.back(RB).count())
                    ve.wait_ge(s3["yw_act"], b.back(RB).count())
                ve.tensor_reduce(idf[r][:], sel4[u][:], AX_X, ALU.add)
                ve.tensor_reduce(gt[r][:], sel4g[u][:], AX_X, ALU.add).then_inc(s3["gt_dve"], 1)

            def row_ids(b):
                r = b.slot(RB)
                ve.wait_ge(s3["gt_dve"], b.count())
                if b.had(RB):
                    ve.wait_ge(put[r], b.back(RB).dma(RB))
                tt(idi[r][:], idf[r][:], pen[:, bass.ds(b.val(), 1)], ALU.add).then_inc(s3["id_dve"], 1)

            def hidden_bias(b):
                u = b.slot(2)
                ex = expert(b)
                ve.wait_ge(s3["h_mm"], b.count())
                if b.had(2):
                    ve.wait_ge(s3["hg_act"], b.back(2).count())
                tt(hb[u][:], bank[1 + u][:, :], b1s[:, bass.ds(ex, 1), :].rearrange("p o f -> p (o f)"),
                   ALU.add).then_inc(s3["hb_dve"], 1)

            def out_bias(b):
                u = b.slot(2)
                ex = expert(b)
                ve.wait_ge(s3["yb_mm"], b.count())
                if b.had(2):
                    ve.wait_ge(s3["yw_act"], b.back(2).count())
                tt(yb[u][:], bank[5 + u][:, 0:D], b2s[:, bass.ds(ex, 1), :].rearrange("p o f -> p (o f)"),
                   ALU.add).then_inc(s3["yb_dve"], 1)

            def step3(s):
                for fn, lag in ((out_bias, LAG3), (row_ids, 2), (ids, 0), (hidden_bias, 0)):
                    if s.back(lag).live(NBP):
                        fn(s.back(lag))

            ve.wait_ge(ld["b1"], 16)
            ve.wait_ge(ld["b2"], 16)
            run_steps(ve, step3, NBP, 4, LO3, N3, load_experts)

            def fin_sum(t):
                b = t.slot(2)
                ve.wait_ge(y4in[t.slot(4)], t.dma(4))
                ve.tensor_reduce(s4[b][:], y4[t.slot(4)][:].rearrange("p k d -> p d k"), AX_X, ALU.add).then_inc(sf["c_fin"], 1)
                ve.wait_ge(sf["c_fin"], t.val(4, 1))
                if t.had(2):
                    ve.wait_ge(sf["s_fin"], t.back(2).count())
                tt(r4[b][:], s4[b][:], x2_all[:, bass.ds(t.val(), 1), :].rearrange("p o d -> p (o d)"),
                   ALU.add).then_inc(sf["c_fin"], 1)
                ve.wait_ge(sf["c_fin"], t.val(4, 2))
                ve.bn_stats(bn4[b][:], r4[b][:]).then_inc(sf["c_fin"], 1)
                wait_apart(ve, [(sf["c_fin"], t.val(4, 3))], clr, 1)
                ve.bn_aggr(mv4[b][:], bn4[b][:]).then_inc(sf["c_fin"], 1)
                ve.wait_ge(sf["c_fin"], t.val(4, 4))
                ts_(ve4[b][:], mv4[b][:, 1:2], EPS_LN, None, ALU.add).then_inc(sf["ve_fin"], 1)

            def fin_norm(t):
                b = t.slot(2)
                ve.wait_ge(sf["pow_fin"], t.count())
                if t.had(2):
                    ve.wait_ge(oout[b], t.back(2).dma(2))
                ts_(o4[b][:], r4[b][:], mv4[b][:, 0:1], rv4[b][:, 0:1], ALU.subtract, ALU.mult).then_inc(sf["s_fin"], 1)

            def step4(s):
                for fn, lag in ((fin_sum, 0), (fin_norm, 1)):
                    if s.back(lag).live(NT):
                        fn(s.back(lag))

            run_steps(ve, step4, NT, 4, 4, NT + 1)

        @block.scalar
        def _(ac):
            act, cp = ac.activation, ACT.Copy

            ac.wait_ge(ld["small"], 16)
            act(expA[:], sm("A_log"), ACT.Exp).then_inc(s0a, 1)
            ac.wait_ge(s0v, 2)
            act(dte[:], dta[:], ACT.Exp).then_inc(s0a, 1)
            ac.wait_ge(s0a, 2)
            ac.wait_ge(ld["cst"], 16)
            act(dtl[:], dte[:], ACT.Ln, bias=c("ones")[:, 0:1]).then_inc(s0a, 1)
            ac.wait_ge(dec_mm, 1)
            act(fC[:].rearrange("p t h -> p (t h)"), bank[3][:, 0:256], ACT.Exp).then_inc(s0a, 1)
            act(fE[:], bank[3][:, 0:256], ACT.Exp, scale=-1.0).then_inc(s0a, 1)
            ac.wait_ge(s0v, 7)
            act(gx[:], gs[:], ACT.Exp, scale=0.5).then_inc(s0a, 1)

            def x_copy(t):
                if t.had(2):
                    ac.wait_ge(s1["xz_mm"], t.back(2).count())
                act(xT[t.slot(2)][:], xT_all[:, bass.ds(t.val(P), P)], cp).then_inc(s1["xt_cp"], 1)

            def block_diag(t):
                b = t.slot(2)
                ac.wait_ge(s1["tr_mm"], t.count())
                if t.had(2):
                    ac.wait_ge(s1["y_mm"], t.back(2).count())
                    ac.wait_ge(s1["sc1_mm"], t.back(2).count())
                act(cb[b][:].rearrange("p k t -> p (k t)"), bank[2][:, :], cp).then_inc(s1["cb_act"], 1)
                for j in range(2):
                    for h in range(HH):
                        m = act(cbd[b][j][:, :, h, :], bank[2][:, j * P:(j + 1) * P].rearrange("p (q i) -> p q i", q=NC),
                                cp, scale=c("head8")[:, h:h + 1])
                m.then_inc(s1["bd_act"], 1)

            def yT_copy(t):
                ac.wait_ge(s1["yt_mm"], t.count())
                if t.had(2):
                    ac.wait_ge(s1["wo_mm"], t.back(2).count())
                act(yT[t.slot(2)][:], bank[6][:, 0:P], cp).then_inc(s1["yt_act"], 1)

            def square(t):
                b = t.slot(2)
                ac.wait_ge(s1["y_add"], t.count())
                if t.had(2):
                    ac.wait_ge(s1["ms_dve"], t.back(2).count())
                act(ysq[b][:], yr[b][:], ACT.Square, accum_out=ss[b][:, 0:1]).then_inc(s1["sq_act"], 1)

            def exp_z(t):
                b = t.slot(2)
                ac.wait_ge(s1["xz_dve"], t.count())
                if t.had(2):
                    ac.wait_ge(s1["c_sil"], t.back(2).val(2, 1))
                act(ez[b][:], z[b][:], ACT.Exp, scale=-1.0).then_inc(s1["ez_act"], 1)

            def x2_copy(t):
                b = t.slot(2)
                ac.wait_ge(s1["x2t_mm"], t.count())
                if t.had(2):
                    ac.wait_ge(s1["lg_mm"], t.back(2).count())
                    ac.wait_ge(s1["lg_dve"], t.back(2).count())
                act(x2T[b][:], bank[6][:, P:2 * P], cp).then_inc(s1["x2t_act"], 1)
                act(x2sq[b][:], x2[b][:], ACT.Square, accum_out=xsq[b][:, 0:1])
                act(x2_all[:, bass.ds(t.val(), 1), :].rearrange("p o d -> p (o d)"), x2[b][:],
                    cp).then_inc(s1["x2c_act"], 1)

            def gate_exp(t):
                b = t.slot(2)
                ac.wait_ge(s1["gate_dve"], t.count())
                if t.had(2):
                    ac.wait_ge(s1["c_rb"], t.back(2).val(5, 5))
                act(ge[b][:], v8[b][:, 0:TOPK], ACT.Exp, bias=nv[b][:, 0:1], accum_out=gsum[b][:, 0:1]).then_inc(s1["ge_act"], 1)

            def step(s):
                for fn, lag in ((block_diag, 1), (x_copy, -1), (gate_exp, 5), (yT_copy, 3), (square, 2),
                                (exp_z, 0), (x2_copy, 4)):
                    if s.back(lag).live(NT):
                        fn(s.back(lag))

            ac.wait_ge(ld["xT"], 16)
            x_copy(Step(0, 2, 0, True))
            run_steps(ac, step, NT - 2, 2, LO1, N1)

            def bt_copy(b):
                ac.wait_ge(s3["bt_mm"], b.count())
                if b.had(2):
                    ac.wait_ge(s3["h_mm"], b.back(2).count())
                act(xbT[b.slot(2)][:], bank[0][:, 0:P], cp).then_inc(s3["bt_act"], 1)

            def gelu(b):
                u = b.slot(2)
                ac.wait_ge(s3["hb_dve"], b.count())
                if b.had(2):
                    ac.wait_ge(s3["ht_mm"], b.back(2).count())
                act(hg[u][:], hb[u][:], ACT.Gelu).then_inc(s3["hg_act"], 1)

            def ht_copy(b):
                u = b.slot(2)
                ac.wait_ge(s3["ht_mm"], b.count())
                if b.had(2):
                    ac.wait_ge(s3["yb_mm"], b.back(2).count())
                act(hT[u][:], bank[3 + u][:, :], cp).then_inc(s3["ht_act"], 1)

            def weigh(b):
                u, r = b.slot(2), b.slot(RB)
                ac.wait_ge(s3["yb_dve"], b.count())
                ac.wait_ge(s3["gt_dve"], b.count())
                if b.had(RB):
                    ac.wait_ge(put[r], b.back(RB).dma(RB))
                act(yw[r][:], yb[u][:], cp, scale=gt[r][:, 0:1]).then_inc(s3["yw_act"], 1)

            def step3(s):
                for fn, lag in ((bt_copy, -1), (ht_copy, 2), (gelu, 0), (weigh, LAG3)):
                    if s.back(lag).live(NBP):
                        fn(s.back(lag))

            bt_copy(Step(0, 4, 0, True))
            run_steps(ac, step3, NBP - 4, 4, LO3, N3)

            def store(t):
                b = t.slot(2)
                ac.wait_ge(sf["s_fin"], t.count())
                ac.dma_start(d["out"][bass.ds(t.val(P), P), :], o4[b][:]).then_inc(oout[b], 16)

            run_steps(ac, store, NT, 2, 2, NT)
            for j in range(2):
                ac.wait_ge(oout[j], 16 * (NT // 2))

        @block.gpsimd
        def _(po):
            po.wait_ge(ld["cst"], 16)
            mhalf = c("mhalf")

            def power(src, dst, ready, done, t):
                po.wait_ge(ready, t.count())
                po.tensor_tensor(dst[t.slot(2)][:], src[t.slot(2)][:], mhalf, ALU.pow).then_inc(done, 1)

            def pow_rms(t):
                if t.had(2):
                    po.wait_ge(s1["yg_dve"], t.back(2).count())
                power(ms, rs, s1["ms_dve"], s1["pow1"], t)

            def pow_ln(t):
                if t.had(2):
                    po.wait_ge(s1["x2_dve"], t.back(2).count())
                power(vre, rv, s1["ve_dve"], s1["pow2"], t)

            def send(t, ks):
                b = t.slot(2)
                wait_apart(po, [(s1["slot_dve"], t.count())], zero_out, 16)
                for k in ks:
                    po.indirect_dma_start(out=xrows, out_offset=bass.IndirectOffsetOnAxis(ap=sli[b][:, k:k + 1], axis=0),
                                          in_=rows[b][:, :], in_offset=None).then_inc(sent[k][b], 16)

            def step(s):
                for fn, lag in ((lambda t: send(t, (0, 1)), 6), (pow_rms, 2), (pow_ln, 3), (lambda t: send(t, (2, 3)), 6)):
                    if s.back(lag).live(NT):
                        fn(s.back(lag))

            po.wait_ge(zero_out, 16)
            run_steps(po, step, NT, 2, LO1, N1)

            def give(b):
                r = b.slot(RB)
                wait_apart(po, [(s3["yw_act"], b.count()), (s3["id_dve"], b.count())], zero_out, 16)
                po.indirect_dma_start(out=yrows, out_offset=bass.IndirectOffsetOnAxis(ap=idi[r][:, 0:1], axis=0),
                                      in_=yw[r][:, :], in_offset=None, bounds_check=S * TOPK - 1,
                                      oob_is_err=False).then_inc(put[r], 16)

            run_steps(po, give, NBP, 4, LO3, NBP)

            def pow_fin(t):
                if t.had(2):
                    po.wait_ge(sf["s_fin"], t.back(2).count())
                power(ve4, rv4, sf["ve_fin"], sf["pow_fin"], t)

            run_steps(po, pow_fin, NT, 2, 2, NT)


_OUT = ((1, 2048, 128), "float32")


def kernel(**inputs):
    import numpy as _np
    import concourse.bacc as _bacc
    from concourse import mybir as _mybir
    from concourse.bass_utils import run_bass_kernel_spmd as _run

    a = {k: _np.asarray(v) for k, v in inputs.items()}
    x = a["L0_attn_x"][0]
    win = a["L0_attn_W_in"]

    def rep(v):
        return _np.broadcast_to(v[None, :], (P, v.shape[0]))

    def flat(v):
        return _np.ascontiguousarray(v)

    host = {
        "consts": const_table()[1],
        "dtlow": flat(_np.concatenate([win[768:784], a["L0_attn_dt_W"].T], 1)),
        "small": flat(_np.concatenate([rep(a["L0_attn_dt_b"]), rep(a["L0_attn_A_log"]), rep(a["L0_attn_D_param"]),
                                       rep(a["L0_ffn_rb"]), a["L0_attn_norm_w"][:, None]], 1)),
        "xT": flat(x.T),
        "x": flat(x.reshape(NT, P, D).transpose(1, 0, 2)),
        "winT": flat(win[0:768].T),
        "woutT": flat(a["L0_attn_W_out"].T),
        "kT": flat(_np.stack([a["L0_ffn_keys"].T, a["L0_ffn_rw"].T], 1)),
        "w1T": flat(a["L0_ffn_w1"].transpose(2, 0, 1)),
        "w2T": flat(a["L0_ffn_w2"].transpose(2, 0, 1).reshape(FB, P, E, D).transpose(1, 2, 0, 3)),
        "b1": flat(a["L0_ffn_b1"].reshape(-1)),
        "b2": flat(a["L0_ffn_b2"].reshape(-1)),
    }
    nc = _bacc.Bacc("TRN2", target_bir_lowering=False, num_devices=1)
    d = {n: nc.dram_tensor(f"in_{n}", v.shape, _mybir.dt.from_np(v.dtype), kind="ExternalInput").ap() for n, v in host.items()}
    d["out"] = nc.dram_tensor("out_0", (S, D), F32, kind="ExternalOutput").ap()
    block_and_moe(nc, d)
    r = _run(nc, [{f"in_{n}": v for n, v in host.items()}], core_ids=[0])
    return r.results[0]["out_0"].reshape(_OUT[0])
```

```python
from contextlib import ExitStack

import numpy as np

import concourse.bass as bass
from concourse import mybir

ALU = mybir.AluOpType
ACT = mybir.ActivationFunctionType
AX_X = mybir.AxisListType.X
F32 = mybir.dt.float32
BF16 = mybir.dt.bfloat16
I32 = mybir.dt.int32
U32 = mybir.dt.uint32

P = 128
D = 128
S = 2048
NT = S // P
H, HD, NS = 16, 8, 16
Q = 64
NC = P // Q
HH = H // 2
E, TOPK, F = 16, 4, 512
FB = F // P
NBLK = S * TOPK // P + E - 1
NBP = NBLK + 1
GT = 2
NG = NT // GT
ROW = D + 3 * TOPK
RA, RI, RG = D, D + TOPK, D + 2 * TOPK
SKIP = float(4 * S * TOPK)
EPS_LN, EPS_RMS = 1e-5, 1e-6


class Step:

    def __init__(self, base, unroll, off, peeled):
        self.base, self.unroll, self.off, self.peeled = base, unroll, off, peeled

    def back(self, k):
        return Step(self.base, self.unroll, self.off - k, self.peeled)

    def val(self, mul=1, add=0):
        fixed = self.off * mul + add
        return fixed if self.peeled else self.base * (self.unroll * mul) + fixed

    def count(self):
        return self.val(1, 1)

    def slot(self, ring):
        return self.off % ring

    def dma(self, ring):
        turn = self.off // ring
        return 16 * (turn + 1) if self.peeled else self.base * (16 * (self.unroll // ring)) + 16 * (turn + 1)

    def live(self, n):
        return not self.peeled or 0 <= self.off < n

    def had(self, k):
        return not self.peeled or self.off >= k


def run_steps(eng, body, n, unroll, lo, last, top=None):
    hi = lo + (n - lo) // unroll * unroll
    for s in range(lo):
        if top and s % unroll == 0:
            top(Step(0, unroll, s, True))
        body(Step(0, unroll, s, True))
    with eng.Fori(lo // unroll, hi // unroll) as i:
        if top:
            top(Step(i, unroll, 0, False))
        for u in range(unroll):
            body(Step(i, unroll, u, False))
    for s in range(hi, last):
        if top and s % unroll == 0:
            top(Step(0, unroll, s, True))
        body(Step(0, unroll, s, True))


def wait_apart(eng, waits, past, past_value):
    waits = [(sem, v if isinstance(v, int) else eng.to_reg(v)) for sem, v in waits]
    eng.wait_ge(past, past_value)
    for sem, v in waits:
        eng.wait_ge(sem, v)


def const_table():
    p = np.arange(P)[:, None]
    cols = {}
    cols["ident"] = np.eye(P)
    same = (p // Q) == (np.arange(P)[None] // Q)
    cols["decay"] = same * ((p <= np.arange(P)[None]) * 1.0 - 0.5)
    cols["chunk0"] = np.repeat((p < Q) * 1.0, P, 1)
    cols["chunk1"] = np.repeat((p >= Q) * 1.0, P, 1)
    cols["before"] = (p < np.arange(P)[None]) * 1.0
    cols["ones"] = np.ones((P, P))
    cols["causal"] = (p % Q <= np.arange(Q)[None]) * 1.0
    cols["head8"] = (p // NS == np.arange(HH)[None]) * 1.0
    cols["head16"] = (p // NS == np.arange(H)[None] % HH) * 1.0
    cols["eids"] = np.tile(np.arange(E), (P, TOPK)) * 1.0
    cols["ebase"] = np.tile(np.arange(E) * S, (P, 1)) * 1.0
    cols["tokid"] = (np.arange(NT)[None] * P + p)[:, :, None] * TOPK + np.arange(TOPK)[None, None] * 1.0
    cols["tokid"] = cols["tokid"].reshape(P, NT * TOPK)
    cols["part"] = p * 1.0
    cols["part128"] = p * 128.0
    cols["mhalf"] = np.full((P, 2), -0.5)
    at, out, n = {}, [], 0
    for k, v in cols.items():
        at[k] = (n, n + v.shape[1])
        n += v.shape[1]
        out.append(v.astype(np.float32))
    return at, np.ascontiguousarray(np.concatenate(out, 1))


SMALL = {"dt_b": (0, 16), "A_log": (16, 32), "D_param": (32, 48), "rb": (48, 64), "norm_w": (64, 65)}


def block_and_moe(nc, d, debug=None):
    at, _ = const_table()
    with ExitStack() as ctx:
        def sb(name, shape, dt=F32):
            return ctx.enter_context(nc.sbuf_tensor(name, shape, dt))

        def sem(name):
            return ctx.enter_context(nc.semaphore(name))

        def sems(name, n):
            return [sem(f"{name}{i}") for i in range(n)]

        cst = sb("cst", [P, at["mhalf"][1]])
        small = sb("small", [P, 65])
        dtlow = sb("dtlow", [16, D + 16])
        xT_all = sb("xT_all", [D, S])
        x_all = sb("x_all", [P, NT, D])
        winT = sb("winT", [D, 768])
        woutT = sb("woutT", [D, D])
        woutn = sb("woutn", [D, D])
        kT = sb("kT", [D, 2, E])
        kw = sb("kw", [D, E])
        ksq = sb("ksq", [D, E])
        kb = sb("kb", [P, E])
        w1s = sb("w1s", [D, E, F + FB])
        w2s = sb("w2s", [P, E, FB, D])
        b2s = sb("b2s", [P, E, D])
        zrow = sb("zrow", [P, ROW])
        shared = sb("shared", [P, 8448])
        used = [0]

        def view(*shape):
            n = int(np.prod(shape))
            a = shared[:, used[0]:used[0] + n]
            used[0] += n
            if len(shape) > 1:
                names = " ".join("abcd"[:len(shape)])
                a = a.rearrange(f"p ({names}) -> p {names}", **dict(zip("abcd", shape)))
            return a

        wdt = sb("wdt", [D, H])
        wxd = sb("wxd", [D, D])
        xd_all, sil_all = sb("xd_all", [P, NT, D]), sb("sil_all", [P, NT, D])
        dtu, dta, dte, dtl, dts, dA = (view(NT * H) for n in range(6))
        expA = sb("expA", [P, H])
        fC = sb("fC", [P, NT, H])
        fE = sb("fE", [P, NT * H])
        fB = sb("fB", [P, NT, H])
        ts, gs, gx = view(NT, NC, H), view(NT * NC, H), view(NT * NC, H)
        gm = sb("gm", [P, NT * NC, H])
        before = sb("before", [P, P], BF16)
        ones16 = sb("ones16", [P, P], BF16)

        def two(name, shape, dt=F32):
            return [sb(f"{name}{i}", shape, dt) for i in range(2)]

        used[0] = 0
        xT = two("xT", [D, P])
        bs = two("bs", [P, H * NS])
        xz = two("xz", [P, NC, D])
        cb = [view(4, P), view(4, P)]
        cbd = [view(2, NC, HH * Q) for i in range(2)]
        sc = [view(H, Q) for i in range(2)]
        st = two("st", [P, 2, D // 2])
        hs = two("hs", [P, NC, 2, D // 2])
        yr, ysq, yg, yT = (two(n, [P, D]) for n in ("yr", "ysq", "yg", "yT"))
        ss, ms, rs = (two(n, [P, 1]) for n in ("ss", "ms", "rs"))
        res = two("res", [P, D])
        bn = two("bn", [P, 6])
        mv, vre, rv = two("mv", [P, 2]), two("vre", [P, 1]), two("rv", [P, 1])
        rows = two("rows", [P, ROW])
        x2 = two("x2", [P, D])
        x2T, x2sq = two("x2T", [D, P]), two("x2sq", [P, D])
        xsq = two("xsq", [P, 1])
        x2_all = x_all
        lg = two("lg", [P, E])
        v8, i8 = two("v8", [P, 8]), two("i8", [P, 8], U32)
        nv, gsum, gr = two("nv", [P, 1]), two("gsum", [P, 1]), two("gr", [P, 1])
        ge = two("ge", [P, TOPK])
        oh = two("oh", [P, TOPK, E])
        ohs = two("ohs", [P, TOPK, E])
        msk, acc = two("msk", [P, E], BF16), two("acc", [P, E], BF16)
        pos = two("pos", [P, E])
        slf, sli = two("slf", [P, TOPK]), two("sli", [P, TOPK], I32)

        cnt, nbf, cum = sb("cnt", [P, E]), sb("nbf", [P, E]), sb("cum", [P, E])
        cnti, nbi = sb("cnti", [P, E], I32), sb("nbi", [P, E], I32)
        cmp_, cnb, eeq, cnn = (sb(n, [P, E]) for n in ("cmp_", "cnb", "eeq", "cnn"))
        ev, ib, nb_ = sb("ev", [P, 1]), sb("ib", [P, 1]), sb("nb_", [P, 1])
        ecl, lo_, t1, t2 = (sb(n, [P, 1]) for n in ("ecl", "lo_", "t1", "t2"))
        stt_ = sb("stt_", [P, 1])
        dg = sb("dg", [P, 4, NBP])
        tb = sb("tb", [P, 4, NBP])
        tbi = sb("tbi", [P, 2, NBP], I32)
        rowat = sb("rowat", [P, NBP])
        rp, g1, g2, pen = (sb(n, [P, NBP]) for n in ("rp", "g1", "g2", "pen"))

        warm = sb("warm", [P, 1])
        RB = 4
        used[0] = 0
        xb = [view(ROW) for i in range(RB)]
        xbT = [view(P), view(P)]
        w1c = [view(F + FB) for i in range(RB)]
        hT = [view(F), view(F)]
        sel4, sel4g = two("sel4", [P, TOPK]), two("sel4g", [P, TOPK])
        idf, gt = ([sb(f"{n}{i}", [P, 1]) for i in range(RB)] for n in ("idf", "gt"))
        idi = [sb(f"idi{i}", [P, 1], I32) for i in range(RB)]
        yb = [view(D), view(D)]
        yw = [view(D) for i in range(RB)]
        w1f, w2f = w1s[:].rearrange("p e f -> p (e f)"), w2s[:].rearrange("p e f d -> p (e f d)")

        def group_view(a, base, g, width):
            n = GT * width
            return a[:, base + g * n:base + (g + 1) * n].rearrange("p (t w) -> p t w", t=GT)

        y4 = [group_view(w1f, 0, g, TOPK * D) for g in range(NG)]
        s4, o4 = ([group_view(w2f, k * NT * D, g, D) for g in range(NG)] for k in range(2))
        bn4, mv4 = sb("bn4", [P, NT, 6]), sb("mv4", [P, NT, 2])
        ve4, rv4, sh4 = (sb(n, [P, NT]) for n in ("ve4", "rv4", "sh4"))

        bank = [ctx.enter_context(nc.psum_tensor(f"bank{i}", [P, 512], F32)) for i in range(8)]

        xrows = nc.dram_tensor("xrows", (E * S, ROW), F32, kind="Internal").ap()
        yrows = nc.dram_tensor("yrows", (S * TOPK, D), F32, kind="Internal").ap()

        def c(name):
            return cst[:, at[name][0]:at[name][1]]

        def sm(name):
            return small[:, SMALL[name][0]:SMALL[name][1]]

        ident = c("ident")
        XD_BANKS, Z_BANKS = (0, 1, 2, 5), (1, 7, 5, 6)

        ld = {k: sem("ld_" + k) for k in "cst small dtlow xT0 xT1 xT2 xT3 win wout k x w1 w2 b2".split()}
        zero_set, zero_out = sem("zero_set"), sem("zero_out")
        wxd_done, xd_mm, xd_cp, z_mm, sil_act = (sem(n) for n in "wxd_done xd_mm xd_cp z_mm sil_act".split())
        wc_mm, wc_cp, dtp_mm, s0v, s0a, dec_mm, gm_done, bf_done = (
            sem(n) for n in "wc_mm wc_cp dtp_mm s0v s0a dec_mm gm_done bf_done".split())
        ksq_done, ksq_mm, kb_done, wo_done0, clr = (sem(n) for n in "ksq_done ksq_mm kb_done wo_done0 clr".split())
        names = ("xt_act pj_mm cbt_mm sc0_mm sc1_mm st_mm yc_mm y_mm yt_mm wo_mm x2t_mm lg_mm pos_mm "
                 "xz_dve y_sc sm0_dve sm1_dve y_add ms_dve yg_dve res_dve ve_dve x2_dve lg_dve oh_dve slot_dve gate_dve row_act "
                 "cb_act bd_act yt_act sq_act b_act x2t_act x2c_act x2k_act ge_act "
                 "pow1 pow2 c_st c_ln c_ra c_rb c_gate h_dve")
        s1 = {n: sem(n) for n in names.split()}
        sent = [sems(f"sent{k}", 2) for k in range(TOPK)]
        cnt_mm, c2, tb_mm, tab_done = (sem(n) for n in "cnt_mm c2 tb_mm tab_done".split())
        names3 = "bt_mm h_mm yb_mm bt_act w1_dve ht_act yb_dve yw_act c_id id_dve gt_dve"
        s3 = {n: sem(n) for n in names3.split()}
        got = sems("got", RB)
        put = sems("put", RB)
        names4 = "sum_fin c_fin sh_fin bn_fin ag_fin ve_fin pow_fin o_fin"
        sf = {n: sem(n) for n in names4.split()}
        y4in, oout = sems("y4in", NG), sem("oout")

        block = ctx.enter_context(nc.Block())
        N1, N3 = NT + 6, NBLK + 2
        LO1, LO3 = 8, 8

        def expert_registers(nc, table, engine, before, after):
            held = {}

            def load(first):
                lo = max(0, first.off - before) if first.peeled else first.off - before
                hi = min(NBLK, first.off + 4 + after) if first.peeled else first.off + 4 + after
                _, regs = nc.values_load_multi_w_load_instructions(
                    table[0:1, 0, bass.ds(first.back(first.off - lo).val(), hi - lo)], engines=[engine], min_val=0,
                    max_val=E - 1, skip_runtime_bounds_check_because="the table holds counts cut to E - 1")
                held.clear()
                held.update({lo + k: x for k, x in enumerate(regs)})

            return load, lambda b: held[b.off]

        @block.sync
        def _(sp):
            def load(k, dst, src):
                sp.dma_start(dst, src).then_inc(ld[k], 16)

            load("dtlow", dtlow[:], d["dtlow"])
            for g in range(4):
                load(f"xT{g}", xT_all[:, g * 4 * P:(g + 1) * 4 * P], d["xT"][:, g * 4 * P:(g + 1) * 4 * P])
            for k, dst in (("small", small), ("win", winT), ("cst", cst), ("k", kT), ("wout", woutT), ("x", x_all)):
                load(k, dst[:], d[{"win": "winT", "k": "kT", "wout": "woutT", "cst": "consts"}.get(k, k)])
            sp.wait_ge(zero_set, 1)
            sp.dma_start(xrows.rearrange("(e r) w -> r e w", e=E)[0:P, :, :],
                         zrow[:].unsqueeze(1).broadcast_to([P, E, ROW])).then_inc(zero_out, 16)
            for k, dst, src in (("w1", w1s, "w1T"), ("w2", w2s, "w2T")):
                sp.dma_start(dst[:], d[src]).then_inc(ld[k], 16)
            sp.dma_start(b2s[:].rearrange("p e f -> p (e f)"), d["b2"].partition_broadcast(P)).then_inc(ld["b2"], 16)

            sp.wait_ge(tab_done, 1)
            for k in range(TOPK):
                for j in range(2):
                    sp.wait_ge(sent[k][j], 16 * (NT // 2))

            def rows_in(s):
                b = s
                if not b.live(NBLK):
                    return
                if b.had(RB):
                    sp.wait_ge(s3["bt_mm"], b.back(RB).count())
                    sp.wait_ge(s3["gt_dve"], b.back(RB).count())
                r = sp.value_load(tbi[0:1, 1, bass.ds(b.val(), 1)], min_val=0, max_val=E * S - P)
                sp.dma_start(xb[b.slot(RB)][:], xrows[bass.ds(r, P), :]).then_inc(got[b.slot(RB)], 16)

            run_steps(sp, rows_in, NBLK, 4, LO3, NBLK)

            for j in range(RB):
                sp.wait_ge(put[j], 16 * ((NBLK + RB - 1 - j) // RB))

            for g in range(NG):
                sp.dma_start(y4[g], yrows.rearrange("(g t p k) d -> g p t (k d)", g=NG, t=GT, k=TOPK)[g]
                             ).then_inc(y4in[g], 16)

        @block.tensor
        def _(pe):
            mm = pe.matmul
            pe.wait_ge(ld["dtlow"], 16)
            mm(bank[5][:, 0:H], dtlow[:, 0:D], dtlow[:, D:D + H], start=True, stop=True).then_inc(wc_mm, 1)
            pe.wait_ge(wc_cp, 1)
            for t in range(NT):
                if t % 4 == 0:
                    pe.wait_ge(ld[f"xT{t // 4}"], 16)
                m = mm(bank[6][:, t * H:(t + 1) * H], xT_all[:, t * P:(t + 1) * P], wdt[:, :], start=True, stop=True)
            m.then_inc(dtp_mm, 1)
            pe.wait_ge(wxd_done, 1)
            for t in range(NT):
                m = mm(bank[XD_BANKS[t // 4]][:, t % 4 * D:(t % 4 + 1) * D], xT_all[:, t * P:(t + 1) * P], wxd[:, :],
                       start=True, stop=True)
                if t % 4 == 3:
                    m.then_inc(xd_mm, 1)
            pe.wait_ge(ksq_done, 1)
            pe.wait_ge(ld["cst"], 16)
            mm(bank[7][:, 0:E], c("ones"), ksq[:, :], start=True, stop=True).then_inc(ksq_mm, 1)
            pe.wait_ge(s0v, 5)
            mm(bank[3][:, 0:NT * H], c("decay"), dA[:, :], start=True, stop=True)
            mm(bank[4][:, 0:256], c("chunk0"), dA[:, :], start=True, stop=True)
            mm(bank[4][:, 256:512], c("chunk1"), dA[:, :], start=True, stop=True).then_inc(dec_mm, 1)
            pe.wait_ge(xd_cp, 4)
            pe.wait_ge(kb_done, 1)
            for t in range(NT):
                m = mm(bank[Z_BANKS[t // 4]][:, t % 4 * D:(t % 4 + 1) * D], xT_all[:, t * P:(t + 1) * P],
                       winT[:, 640:768], start=True, stop=True)
                if t % 4 == 3:
                    m.then_inc(z_mm, 1)

            def bank_of_z(t, n):
                if t.peeled and t.off == 0:
                    pe.wait_ge(sil_act, n)

            def project_cb(t):
                if t.had(1):
                    pe.wait_ge(s1["bd_act"], t.back(1).count())
                for k, c0 in enumerate((384, 512, 128, 256)):
                    m = mm(bank[2][:, k * P:(k + 1) * P], winT[:, c0:c0 + P], xT_all[:, bass.ds(t.val(P), P)],
                           start=True, stop=True)
                m.then_inc(s1["cbt_mm"], 1)

            def y_transpose(t):
                bank_of_z(t, 4)
                pe.wait_ge(s1["yg_dve"], t.count())
                if t.had(2):
                    pe.wait_ge(s1["x2t_act"], t.back(2).count())
                pe.transpose(bank[6][:, 0:P], yg[t.slot(2)][:, :], ident).then_inc(s1["yt_mm"], 1)

            def y_cross(t):
                b = t.slot(2)
                bank_of_z(t, 3)
                pe.wait_ge(s1["h_dve"], t.val(NC, 1))
                pe.wait_ge(s1["cb_act"], t.count())
                if t.had(1):
                    pe.wait_ge(s1["y_sc"], t.back(1).count())
                for j in range(2):
                    for q in range(NC):
                        m = mm(bank[5][q * Q:(q + 1) * Q, j * 64:(j + 1) * 64], cb[b][:, j, q * Q:(q + 1) * Q],
                               hs[b][:, q, j, :], start=(j == 0), stop=False, skip_group_check=True)
                m.then_inc(s1["yc_mm"], 1)

            def y_intra(t, quarter):
                b = t.slot(2)
                for h in range(quarter * 4, quarter * 4 + 4):
                    if h % HH == 0:
                        wait_apart(pe, [(s1[f"sm{h // HH}_dve"], t.count())], gm_done, 1)
                    for q in range(NC):
                        r = slice(q * Q, (q + 1) * Q)
                        m = mm(bank[5][r, h * HD:(h + 1) * HD], sc[b][r, h, :], xz[b][r, q, h * HD:(h + 1) * HD],
                               start=False, stop=(h == H - 1), skip_group_check=True)
                if quarter == 3:
                    m.then_inc(s1["y_mm"], 1)

            def project(t):
                b = t.slot(2)
                pe.wait_ge(s1["xt_act"], t.count())
                if t.had(2):
                    pe.wait_ge(s1["b_act"], t.back(2).count())
                bank_of_z(t.back(1), 1)
                mm(bank[b][:, 0:384], xT[b][:, :], winT[:, 0:384], start=True, stop=True).then_inc(s1["pj_mm"], 1)

            def tail_read(s):
                for done, t, mul, add in ((s1["res_dve"], s.back(4), 1, 1), (s1["lg_dve"], s.back(5), 1, 1),
                                          (s1["c_rb"], s.back(6), 5, 2)):
                    if t.live(NT):
                        pe.wait_ge(done, t.val(mul, add))

            def states(t):
                b = t.slot(2)
                bank_of_z(t, 2)
                tail_read(t.back(-1))
                pe.wait_ge(s1["b_act"], t.count())
                if t.had(1):
                    pe.wait_ge(s1["c_st"], t.val(NC))
                for j in range(2):
                    m = mm(bank[7][:, j * P:(j + 1) * P], bs[b][:, j * P:(j + 1) * P],
                           xz[b][:, :, j * 64:(j + 1) * 64], start=True, stop=True)
                m.then_inc(s1["st_mm"], 1)

            def tail_free(s):
                if s.back(1).live(NT):
                    pe.wait_ge(s1["c_st"], s.back(1).val(NC, NC))
                else:
                    tail_read(s)

            def out_product(t):
                tail_free(t.back(-3))
                pe.wait_ge(s1["yt_act"], t.count())
                mm(bank[7][:, 256:384], yT[t.slot(2)][:, :], woutn[:, :], start=True, stop=True).then_inc(s1["wo_mm"], 1)

            def scores(t, j):
                pe.wait_ge(s1["bd_act"], t.count())
                if t.had(1):
                    pe.wait_ge(s1[f"sm{j}_dve"], t.back(1).count())
                b = t.slot(2)
                for q in range(NC):
                    m = mm(bank[3 + j][q * Q:(q + 1) * Q, :], cb[b][:, 2 + j, q * Q:(q + 1) * Q],
                           cbd[b][:, j, q, :].rearrange("p (h i) -> p h i", h=HH).rearrange("p h i -> p (h i)"),
                           start=True, stop=True, skip_group_check=True)
                m.then_inc(s1[f"sc{j}_mm"], 1)

            def x2_transpose(t):
                pe.wait_ge(s1["x2_dve"], t.count())
                if t.had(0):
                    nxt = t.back(-1)
                    if nxt.live(NT):
                        pe.wait_ge(s1["yt_act"], nxt.count())
                pe.transpose(bank[6][:, P:2 * P], x2[t.slot(2)][:, :], ident).then_inc(s1["x2t_mm"], 1)

            def router(t):
                if t.peeled and not t.back(-1).live(NT):
                    tail_free(t.back(-4))
                pe.wait_ge(s1["x2t_act"], t.count())
                mm(bank[7][:, 384:384 + E], x2T[t.slot(2)][:, :], kw[:, :], start=True, stop=True).then_inc(s1["lg_mm"], 1)

            def positions(t):
                b = t.slot(2)
                if t.peeled and not t.back(-1).live(NT):
                    tail_free(t.back(-5))
                pe.wait_ge(s1["oh_dve"], t.count())
                if t.had(1):
                    pe.wait_ge(s1["c_rb"], t.back(1).val(5, 2))
                mm(bank[7][:, 400:400 + E], before[:, :], msk[b][:, :], start=True, stop=False)
                mm(bank[7][:, 400:400 + E], ones16[:, :], acc[b][:, :], start=False, stop=True).then_inc(s1["pos_mm"], 1)

            def step(s):
                order = ((project, 0), (project_cb, 0), (y_cross, 2), (lambda t: y_intra(t, 0), 2), (states, 1),
                         (lambda t: y_intra(t, 1), 2), (lambda t: scores(t, 0), 1), (y_transpose, 3),
                         (lambda t: y_intra(t, 2), 2), (lambda t: scores(t, 1), 1), (x2_transpose, 4),
                         (lambda t: y_intra(t, 3), 2), (out_product, 3), (router, 4), (positions, 5))
                for fn, lag in order:
                    if s.back(lag).live(NT):
                        fn(s.back(lag))

            pe.wait_ge(ld["win"], 16)
            run_steps(pe, step, NT, 2, LO1, N1)

            pe.wait_ge(s1["c_rb"], (NT - 1) * 5 + 1)
            mm(bank[0][:, 0:E], ones16[:, :], acc[NT % 2][:, :], start=True, stop=True).then_inc(cnt_mm, 1)
            pe.wait_ge(c2, 18)
            mm(bank[0][:, 64:64 + 4 * NBP], c("ones"), dg[:].rearrange("p k b -> p (k b)"),
               start=True, stop=True).then_inc(tb_mm, 1)

            load_experts, expert = expert_registers(nc, tbi, mybir.EngineType.PE, 2, 0)

            def rows_transpose(b):
                pe.wait_ge(got[b.slot(RB)], b.dma(RB))
                if b.had(1):
                    pe.wait_ge(s3["bt_act"], b.back(1).count())
                pe.transpose(bank[0][:, 0:P], xb[b.slot(RB)][:, 0:D], ident).then_inc(s3["bt_mm"], 1)

            def hidden(b):
                u, w = b.slot(2), w1c[b.slot(RB)]
                pe.wait_ge(s3["bt_act"], b.count())
                pe.wait_ge(s3["w1_dve"], b.count())
                if b.had(2):
                    pe.wait_ge(s3["ht_act"], b.back(2).count())
                for f in range(FB):
                    m = mm(bank[1 + u][:, f * P:(f + 1) * P], w[:, f * P:(f + 1) * P], xbT[u][:, :], start=True, stop=True)
                m.then_inc(s3["h_mm"], 1)

            def expert_out(b):
                u = b.slot(2)
                ex = expert(b)
                pe.wait_ge(s3["ht_act"], b.count())
                if b.had(2):
                    pe.wait_ge(s3["yb_dve"], b.back(2).count())
                for f in range(FB):
                    m = mm(bank[5 + u][:, 0:D], hT[u][:, f * P:(f + 1) * P], w2s[:, bass.ds(ex, 1), f, :],
                           start=(f == 0), stop=(f == FB - 1))
                m.then_inc(s3["yb_mm"], 1)

            def step3(s):
                for fn, lag in ((expert_out, 2), (rows_transpose, -1), (hidden, 0)):
                    if s.back(lag).live(NBLK):
                        fn(s.back(lag))

            pe.wait_ge(tab_done, 1)
            pe.wait_ge(ld["w1"], 16)
            pe.wait_ge(ld["w2"], 16)
            rows_transpose(Step(0, 4, 0, True))
            run_steps(pe, step3, NBLK - 4, 4, LO3, N3, load_experts)

            pe.wait_ge(s3["bt_act"], NBLK)
            pe.wait_ge(s3["ht_act"], NBLK)
            pe.wait_ge(s3["yb_dve"], NBLK)
            for g in range(NG):
                mm(bank[g][:, 0:GT * D].rearrange("p (t d) -> p t d", t=GT), ident,
                   x2_all[:, g * GT:(g + 1) * GT, :], start=True, stop=False)
            for g in range(NG):
                pe.wait_ge(y4in[g], 16)
                for k in (2, 3):
                    mm(bank[g][:, 0:GT * D].rearrange("p (t d) -> p t d", t=GT), ident,
                       y4[g][:, :, k * D:(k + 1) * D], start=False, stop=False)
                pe.wait_ge(sf["c_fin"], g + 1)
                mm(bank[g][:, 0:GT * D].rearrange("p (t d) -> p t d", t=GT), ident, s4[g],
                   start=False, stop=True).then_inc(sf["sum_fin"], 1)

        @block.vector
        def _(ve):
            tt, ts_, stt = ve.tensor_tensor, ve.tensor_scalar, ve.scalar_tensor_tensor

            ve.memset(zrow[:], 0.0).then_inc(zero_set, 1)
            for i in range(2):
                ve.memset(xz[i][:], 0.0)
                ve.memset(acc[i][:], 0.0)
                ve.memset(hs[i][:], 0.0)
            ve.memset(gs[:, NT * NC - 1, :], 0.0).then_inc(clr, 1)
            ve.wait_ge(wc_mm, 1)
            ve.tensor_copy(wdt[:], bank[5][:, 0:H]).then_inc(wc_cp, 1)
            ve.wait_ge(ld["small"], 16)
            ve.wait_ge(ld["win"], 16)
            tt(wxd[:].rearrange("p (h w) -> p h w", h=H), winT[:, 0:D].rearrange("p (h w) -> p h w", h=H),
               sm("D_param").unsqueeze(2).broadcast_to([P, H, HD]), ALU.mult).then_inc(wxd_done, 1)
            ve.wait_ge(ld["k"], 16)
            tt(ksq[:], kT[:, 0, :], kT[:, 0, :], ALU.mult).then_inc(ksq_done, 1)
            stt(out=kw[:], in0=kT[:, 0, :], scalar=2.0, in1=kT[:, 1, :], op0=ALU.mult, op1=ALU.add)
            ve.wait_ge(ld["cst"], 16)
            ve.tensor_copy(before[:], c("before"))
            ve.tensor_copy(ones16[:], c("ones")).then_inc(bf_done, 1)
            ve.wait_ge(ld["small"], 16)
            ve.wait_ge(dtp_mm, 1)

            def v3(a):
                return a[:].rearrange("p (t h) -> p t h", t=NT)

            def over_tiles(a):
                return a.unsqueeze(1).broadcast_to([P, NT, H])

            tt(v3(dtu), bank[6][:, 0:NT * H].rearrange("p (t h) -> p t h", t=NT), over_tiles(sm("dt_b")),
               ALU.add).then_inc(s0v, 1)
            ve.wait_ge(s0v, 1)
            stt(out=dta[:], in0=dtu[:], scalar=-1.0, in1=dtu[:], op0=ALU.mult, op1=ALU.min).then_inc(s0v, 1)

            def take_xd(g):
                ve.wait_ge(xd_mm, g + 1)
                ve.tensor_copy(xd_all[:, g * 4:(g + 1) * 4, :].rearrange("p t d -> p (t d)"),
                               bank[XD_BANKS[g]][:, :]).then_inc(xd_cp, 1)

            for g in range(3):
                take_xd(g)
            ve.wait_ge(ksq_mm, 1)
            tt(kb[:], sm("rb"), bank[7][:, 0:E], ALU.subtract).then_inc(kb_done, 1)
            ve.wait_ge(ld["wout"], 16)
            ts_(woutn[:], woutT[:], sm("norm_w"), None, ALU.mult).then_inc(wo_done0, 1)
            ve.wait_ge(s0a, 3)
            stt(out=dts[:], in0=dtu[:], scalar=0.0, in1=dtl[:], op0=ALU.max, op1=ALU.add).then_inc(s0v, 1)
            ve.wait_ge(s0v, 3)
            stt(out=v3(dA), in0=v3(dts), scalar=-1.0, in1=over_tiles(expA[:]), op0=ALU.mult,
                op1=ALU.mult).then_inc(s0v, 2)
            take_xd(3)
            ve.wait_ge(dec_mm, 1)
            for q in range(NC):
                m = ve.tensor_copy(ts[:, :, q, :], bank[4][:, q * 256:(q + 1) * 256].rearrange("p (t h) -> p t h", t=NT))
            m.then_inc(s0v, 1)
            ve.wait_ge(s0v, 6)
            ve.wait_ge(clr, 1)
            tsq = ts[:].rearrange("p t q h -> p (t q) h")
            tt(gs[:, 0:NT * NC - 1, :], tsq[:, 0:NT * NC - 1, :], tsq[:, 1:NT * NC, :], ALU.add).then_inc(s0v, 1)
            ve.wait_ge(s0a, 5)
            tt(fB[:].rearrange("p t h -> p (t h)"), dts[:], fE[:], ALU.mult)
            ve.wait_ge(s0a, 6)
            tt(gm[:], gx[:], c("head16").unsqueeze(1).broadcast_to([P, NT * NC, H]), ALU.mult).then_inc(gm_done, 1)
            ve.wait_ge(gm_done, 1)

            def y_scale(t):
                b = t.slot(2)
                ve.wait_ge(s1["y_mm"], t.count())
                if t.had(2):
                    ve.wait_ge(s1["yg_dve"], t.back(2).count())
                    ve.wait_ge(s1["sq_act"], t.back(2).count())
                tt(by_head(yr[b][:]), by_head(bank[5][:, 0:D]), factor(fC, t), ALU.mult).then_inc(s1["y_sc"], 1)

            def y_add(t):
                b = t.slot(2)
                ve.wait_ge(s1["y_sc"], t.count())
                tt(yr[b][:], yr[b][:], of_tile(xd_all, t), ALU.add).then_inc(s1["y_add"], 1)

            def of_tile(a, t):
                return a[:, bass.ds(t.val(), 1), :].rearrange("p o d -> p (o d)")

            def by_head(a):
                return a.rearrange("p (h w) -> p h w", h=H)

            def factor(f, t, r=slice(0, P)):
                return f[r, bass.ds(t.val(), 1), :].rearrange("p o h -> p (o h)").unsqueeze(2).broadcast_to(
                    [r.stop - r.start, H, HD])

            def take_x(t):
                b = t.slot(2)
                ve.wait_ge(s1["pj_mm"], t.count())
                if t.had(2):
                    ve.wait_ge(s1["y_mm"], t.back(2).count())
                for q in range(NC):
                    r = slice(q * Q, (q + 1) * Q)
                    m = tt(by_head(xz[b][r, q, :]), by_head(bank[b][r, 0:D]), factor(fB, t, r), ALU.mult)
                m.then_inc(s1["xz_dve"], 1)

            def states_after(t, q):
                return hs[t.slot(2)][:, 1, :, :] if q == 0 else hs[1 - t.slot(2)][:, 0, :, :]

            def carry_sum(t, q):
                b = t.slot(2)
                sv = bank[7][:, 0:2 * P].rearrange("p (j q w) -> p j q w", j=2, q=NC)
                if q == 0:
                    ve.wait_ge(s1["st_mm"], t.count())
                if q == 1 or t.had(1):
                    ve.wait_ge(s1["h_dve"], t.val(NC, q))
                tt(st[q][:], hs[b][:, q, :, :], sv[:, :, q, :], ALU.add).then_inc(s1["c_st"], 1)

            def carry_scale(t, q):
                if q == 1 and t.had(1):
                    ve.wait_ge(s1["yc_mm"], t.back(1).count())
                if q == 0 and t.had(2):
                    ve.wait_ge(s1["yc_mm"], t.back(2).count())
                ve.wait_ge(s1["c_st"], t.val(NC, q + 1))
                g = gm[:, bass.ds(t.val(NC, q), 1), :].rearrange("p o h -> p (o h)").unsqueeze(2)
                tt(states_after(t, q).rearrange("p j (h w) -> p (j h) w", h=HH),
                   st[q][:].rearrange("p j (h w) -> p (j h) w", h=HH),
                   g.broadcast_to([P, H, HD]), ALU.mult).then_inc(s1["h_dve"], 1)

            def residual(t):
                b = t.slot(2)
                for done, lag in ((s1["pos_mm"], 2), (s1["lg_mm"], 1), (s1["wo_mm"], 0)):
                    if t.back(lag).live(NT):
                        ve.wait_ge(done, t.back(lag).count())
                        break
                if t.had(2):
                    ve.wait_ge(s1["x2_dve"], t.back(2).count())
                tt(res[b][:], bank[7][:, 256:384], x_all[:, bass.ds(t.val(), 1), :].rearrange("p o d -> p (o d)"),
                   ALU.add).then_inc(s1["res_dve"], 1)

            def res_stats(t):
                ve.wait_ge(s1["res_dve"], t.count())
                ve.bn_stats(bn[t.slot(2)][:], res[t.slot(2)][:]).then_inc(s1["c_ln"], 1)

            def res_moments(t):
                wait_apart(ve, [(s1["c_ln"], t.val(2, 1))], clr, 1)
                ve.bn_aggr(mv[t.slot(2)][:], bn[t.slot(2)][:]).then_inc(s1["c_ln"], 1)

            def res_var(t):
                ve.wait_ge(s1["c_ln"], t.val(2, 2))
                if t.had(2):
                    ve.wait_ge(s1["pow2"], t.back(2).count())
                ts_(vre[t.slot(2)][:], mv[t.slot(2)][:, 1:2], EPS_LN, None, ALU.add).then_inc(s1["ve_dve"], 1)

            def causal(t, j):
                b = t.slot(2)
                ve.wait_ge(s1[f"sc{j}_mm"], t.count())
                if t.had(2):
                    ve.wait_ge(s1["y_mm"], t.back(2).count())
                tt(sc[b][:, j * HH:(j + 1) * HH, :], bank[3 + j][:, :].rearrange("p (h i) -> p h i", h=HH),
                   c("causal").unsqueeze(1).broadcast_to([P, HH, Q]), ALU.mult).then_inc(s1[f"sm{j}_dve"], 1)

            def mean_square(t):
                b = t.slot(2)
                ve.wait_ge(s1["sq_act"], t.count())
                if t.had(2):
                    ve.wait_ge(s1["pow1"], t.back(2).count())
                ts_(ms[b][:], ss[b][:], 1.0 / D, EPS_RMS, ALU.mult, ALU.add).then_inc(s1["ms_dve"], 1)

            def gated(t):
                b = t.slot(2)
                ve.wait_ge(s1["pow1"], t.count())
                if t.peeled and t.off == 0:
                    ve.wait_ge(sil_act, 4)
                if t.had(2):
                    ve.wait_ge(s1["yt_mm"], t.back(2).count())
                stt(out=yg[b][:], in0=yr[b][:], scalar=rs[b][:, 0:1], in1=of_tile(sil_all, t), op0=ALU.mult,
                    op1=ALU.mult).then_inc(s1["yg_dve"], 1)

            def normed(t):
                b = t.slot(2)
                ve.wait_ge(s1["pow2"], t.count())
                if t.had(2):
                    ve.wait_ge(s1["x2t_mm"], t.back(2).count())
                    ve.wait_ge(s1["x2c_act"], t.back(2).count())
                    ve.wait_ge(s1["x2k_act"], t.back(2).count())
                ts_(x2[b][:], res[b][:], mv[b][:, 0:1], rv[b][:, 0:1], ALU.subtract,
                    ALU.mult).then_inc(s1["x2_dve"], 1)

            def logits(t):
                b = t.slot(2)
                for done, lag in ((s1["pos_mm"], 1), (s1["lg_mm"], 0)):
                    if t.back(lag).live(NT):
                        ve.wait_ge(done, t.back(lag).count())
                        break
                ve.wait_ge(s1["x2c_act"], t.count())
                stt(out=lg[b][:], in0=bank[7][:, 384:384 + E], scalar=xsq[b][:, 0:1], in1=kb[:], op0=ALU.subtract,
                    op1=ALU.add).then_inc(s1["lg_dve"], 1)

            def best(t):
                b = t.slot(2)
                used = [(s1["ge_act"], t.back(2).count())] if t.had(2) else []
                wait_apart(ve, used + [(s1["lg_dve"], t.count())], clr, 1)
                ve.max(v8[b][:], lg[b][:]).then_inc(s1["c_ra"], 1)

            def best_ids(t):
                b = t.slot(2)
                wait_apart(ve, [(s1["c_ra"], t.val(3, 1))], clr, 1)
                ve.max_index(i8[b][:], v8[b][:], lg[b][:]).then_inc(s1["c_ra"], 1)
                ts_(nv[b][:], v8[b][:, 0:1], -1.0, None, ALU.mult).then_inc(s1["gate_dve"], 1)

            def one_hot(t):
                b = t.slot(2)
                ve.wait_ge(s1["c_ra"], t.val(3, 2))
                tt(oh[b][:], c("eids").rearrange("p (k e) -> p k e", k=TOPK),
                   i8[b][:, 0:TOPK].unsqueeze(2).broadcast_to([P, TOPK, E]), ALU.is_equal).then_inc(s1["c_ra"], 1)

            def chosen(t):
                b = t.slot(2)
                ve.wait_ge(s1["c_ra"], t.val(3, 3))
                if t.had(2):
                    ve.wait_ge(s1["pos_mm"], t.back(2).count())
                with nc.allow_low_precision("0/1 values"):
                    ve.tensor_reduce(msk[b][:], oh[b][:].rearrange("p k e -> p e k"), AX_X, ALU.add).then_inc(s1["oh_dve"], 1)

            def pack_row(t):
                b = t.slot(2)
                if t.had(2):
                    for k in range(TOPK):
                        ve.wait_ge(sent[k][b], t.back(2).dma(2))
                ve.wait_ge(s1["oh_dve"], t.count())
                ve.tensor_copy(rows[b][:, RA:RI], i8[b][:, 0:TOPK])
                ve.tensor_copy(rows[b][:, RI:RG], c("tokid").rearrange("p (t k) -> p t k", t=NT)
                               [:, bass.ds(t.val(), 1), :].rearrange("p o k -> p (o k)"))

            def place(t):
                b = t.slot(2)
                ve.wait_ge(s1["pos_mm"], t.count())
                if t.had(1):
                    ve.wait_ge(s1["c_rb"], t.val(5))
                tt(acc[1 - b][:], acc[b][:], msk[b][:], ALU.add).then_inc(s1["c_rb"], 1)
                tt(pos[b][:], bank[7][:, 400:400 + E], c("ebase"), ALU.add).then_inc(s1["c_rb"], 1)

            def place_of_chosen(t):
                b = t.slot(2)
                ve.wait_ge(s1["c_rb"], t.val(5, 2))
                tt(ohs[b][:], oh[b][:], pos[b][:].unsqueeze(1).broadcast_to([P, TOPK, E]), ALU.mult).then_inc(s1["c_rb"], 1)

            def gate_inv(t):
                ve.wait_ge(s1["ge_act"], t.count())
                ve.reciprocal(gr[t.slot(2)][:], gsum[t.slot(2)][:]).then_inc(s1["c_gate"], 1)

            def slots(t):
                ve.wait_ge(s1["c_rb"], t.val(5, 3))
                ve.tensor_reduce(slf[t.slot(2)][:], ohs[t.slot(2)][:], AX_X, ALU.add).then_inc(s1["c_rb"], 1)

            def gates(t):
                b = t.slot(2)
                ve.wait_ge(s1["c_gate"], t.count())
                ts_(rows[b][:, RG:ROW], ge[b][:], gr[b][:, 0:1], None, ALU.mult).then_inc(s1["c_rb"], 1)

            def slots_out(t):
                ve.wait_ge(s1["c_rb"], t.val(5, 4))
                ve.tensor_copy(sli[t.slot(2)][:], slf[t.slot(2)][:]).then_inc(s1["slot_dve"], 1)

            def step(s):
                for fn, lag in ((residual, 4), (logits, 5), (place, 6), (res_stats, 4), (best, 5),
                                (place_of_chosen, 6), (mean_square, 3), (res_moments, 4), (best_ids, 5), (slots, 6), (res_var, 4),
                                (one_hot, 5), (gated, 3), (gate_inv, 6), (chosen, 5), (pack_row, 6), (gates, 6),
                                (slots_out, 6), (normed, 4),
                                (lambda t: carry_sum(t, 0), 1), (lambda t: carry_scale(t, 0), 1), (lambda t: carry_sum(t, 1), 1),
                                (lambda t: carry_scale(t, 1), 1),
                                (lambda t: causal(t, 0), 1), (lambda t: causal(t, 1), 1),
                                (y_scale, 2), (take_x, 0), (y_add, 2)):
                    if s.back(lag).live(NT):
                        fn(s.back(lag))

            ve.wait_ge(ld["x"], 16)
            ve.wait_ge(s0a, 6)
            run_steps(ve, step, NT, 2, LO1, N1)

            links = [0]

            def link(ins):
                links[0] += 1
                ins.then_inc(c2, 1)
                ve.wait_ge(c2, links[0])

            def floor128(dst, src):
                link(ts_(cnti[:], src, float(P - 1), None, ALU.add))
                link(ts_(nbi[:], cnti[:], 7, None, ALU.arith_shift_right))
                link(ve.tensor_copy(dst, nbi[:]))

            ve.wait_ge(cnt_mm, 1)
            link(ve.tensor_copy(cnt[:], bank[0][:, 0:E]))
            floor128(nbf[:], cnt[:])
            link(ve.tensor_tensor_scan(cum[:], c("ones")[:, 0:E], nbf[:], 0.0, ALU.mult, ALU.add))
            link(ts_(cmp_[:], cum[:], c("part"), None, ALU.is_le))
            link(ve.tensor_reduce(ev[:], cmp_[:], AX_X, ALU.add))
            link(tt(cnb[:], cmp_[:], nbf[:], ALU.mult))
            link(ve.tensor_reduce(ib[:], cnb[:], AX_X, ALU.add))
            link(ts_(eeq[:], c("eids")[:, 0:E], ev[:, 0:1], None, ALU.is_equal))
            link(tt(cnn[:], eeq[:], cnt[:], ALU.mult))
            link(ve.tensor_reduce(nb_[:], cnn[:], AX_X, ALU.add))
            link(ts_(ecl[:], ev[:], float(E - 1), None, ALU.min))
            link(stt(out=lo_[:], in0=ib[:], scalar=-float(P), in1=c("part128"), op0=ALU.mult, op1=ALU.add))
            link(stt(out=t1[:], in0=nb_[:], scalar=-float(P), in1=lo_[:], op0=ALU.add, op1=ALU.min))
            link(ts_(stt_[:], t1[:], 0.0, None, ALU.max))
            for k, v in enumerate((ecl, stt_, lo_, nb_)):
                m = ts_(dg[:, k, :], ident[:, 0:NBP], v[:, 0:1], None, ALU.mult)
            link(m)
            link(ts_(t2[:], t1[:], 0.0, None, ALU.max))
            ve.wait_ge(tb_mm, 1)
            link(ve.tensor_copy(tb[:].rearrange("p k b -> p (k b)"), bank[0][:, 64:64 + 4 * NBP]))
            link(stt(out=rowat[:], in0=tb[:, 0, :], scalar=float(S), in1=tb[:, 1, :], op0=ALU.mult, op1=ALU.add))
            link(ve.tensor_copy(tbi[:, 0, :], tb[:, 0, :]))
            ve.tensor_copy(tbi[:, 1, :], rowat[:]).then_inc(tab_done, 1)
            link(ts_(rp[:], tb[:, 1, :], c("part"), None, ALU.add))
            link(tt(g1[:], rp[:], tb[:, 2, :], ALU.is_ge))
            link(tt(g2[:], rp[:], tb[:, 3, :], ALU.is_lt))
            link(tt(rp[:], g1[:], g2[:], ALU.mult))
            link(ts_(pen[:], rp[:], -SKIP, SKIP, ALU.mult, ALU.add))

            load_experts, expert = expert_registers(nc, tbi, mybir.EngineType.DVE, 2, 1)

            def ids(b):
                u, r = b.slot(2), b.slot(RB)
                x = xb[r]
                ve.wait_ge(got[r], b.dma(RB))
                if b.had(2):
                    ve.wait_ge(s3["gt_dve"], b.back(2).count())
                eid = tb[:, 0, bass.ds(b.val(), 1)]
                stt(out=sel4[u][:], in0=x[:, RA:RI], scalar=eid, in1=x[:, RI:RG], op0=ALU.is_equal, op1=ALU.mult)
                stt(out=sel4g[u][:], in0=x[:, RA:RI], scalar=eid, in1=x[:, RG:ROW], op0=ALU.is_equal,
                    op1=ALU.mult).then_inc(s3["c_id"], 1)
                ve.wait_ge(s3["c_id"], b.count())
                if b.had(RB):
                    ve.wait_ge(s3["id_dve"], b.back(RB).count())
                    ve.wait_ge(s3["yw_act"], b.back(RB).count())
                ve.tensor_reduce(idf[r][:], sel4[u][:], AX_X, ALU.add)
                ve.tensor_reduce(gt[r][:], sel4g[u][:], AX_X, ALU.add).then_inc(s3["gt_dve"], 1)

            def row_ids(b):
                r = b.slot(RB)
                ve.wait_ge(s3["gt_dve"], b.count())
                if b.had(RB):
                    ve.wait_ge(put[r], b.back(RB).dma(RB))
                tt(idi[r][:], idf[r][:], pen[:, bass.ds(b.val(), 1)], ALU.add).then_inc(s3["id_dve"], 1)

            def take_w1(b):
                r = b.slot(RB)
                if b.had(RB):
                    ve.wait_ge(s3["ht_act"], b.back(RB).count())
                ve.tensor_copy(w1c[r][:], w1s[:, bass.ds(expert(b), 1), :].rearrange("p o f -> p (o f)")
                               ).then_inc(s3["w1_dve"], 1)

            def out_bias(b):
                u = b.slot(2)
                ex = expert(b)
                ve.wait_ge(s3["yb_mm"], b.count())
                if b.had(2):
                    ve.wait_ge(s3["yw_act"], b.back(2).count())
                tt(yb[u][:], bank[5 + u][:, 0:D], b2s[:, bass.ds(ex, 1), :].rearrange("p o f -> p (o f)"),
                   ALU.add).then_inc(s3["yb_dve"], 1)

            def step3(s):
                for fn, lag in ((take_w1, -1), (row_ids, 2), (ids, 0), (out_bias, 2)):
                    if s.back(lag).live(NBLK):
                        fn(s.back(lag))

            ve.wait_ge(ld["w1"], 16)
            ve.wait_ge(ld["b2"], 16)
            load_experts(Step(0, 4, 0, True))
            take_w1(Step(0, 4, 0, True))
            run_steps(ve, step3, NBLK - 4, 4, LO3, N3, load_experts)

            def sums(g):
                ve.wait_ge(y4in[g], 16)
                tt(s4[g], y4[g][:, :, 0:D], y4[g][:, :, D:2 * D], ALU.add).then_inc(sf["c_fin"], 1)

            def stats(g):
                ve.wait_ge(sf["sum_fin"], g + 1)
                for t in range(GT):
                    m = ve.bn_stats(bn4[:, g * GT + t, :], bank[g][:, t * D:(t + 1) * D])
                m.then_inc(sf["bn_fin"], 1)

            def moments(g):
                ve.wait_ge(sf["bn_fin"], g + 1)
                for t in range(GT):
                    m = ve.bn_aggr(mv4[:, g * GT + t, :], bn4[:, g * GT + t, :])
                m.then_inc(sf["ag_fin"], 1)

            def variances(g):
                r = slice(g * GT, (g + 1) * GT)
                ve.wait_ge(sf["ag_fin"], g + 1)
                ts_(ve4[:, r], mv4[:, r, 1:2].rearrange("p t o -> p (t o)"), EPS_LN, None, ALU.add).then_inc(sf["ve_fin"], 1)

            def shifts(g):
                r = slice(g * GT, (g + 1) * GT)
                ve.wait_ge(sf["pow_fin"], g + 1)
                stt(out=sh4[:, r], in0=mv4[:, r, 0:1].rearrange("p t o -> p (t o)"), scalar=-1.0, in1=rv4[:, r],
                    op0=ALU.mult, op1=ALU.mult).then_inc(sf["sh_fin"], 1)

            for g in range(NG + 2):
                for fn, lag in ((sums, 0), (stats, 1), (shifts, 2), (moments, 1), (variances, 1)):
                    if 0 <= g - lag < NG:
                        fn(g - lag)

        @block.scalar
        def _(ac):
            act, cp = ac.activation, ACT.Copy

            def x_copy(t):
                if t.had(2):
                    ac.wait_ge(s1["pj_mm"], t.back(2).count())
                act(xT[t.slot(2)][:], xT_all[:, bass.ds(t.val(P), P)], cp).then_inc(s1["xt_act"], 1)

            ac.wait_ge(ld["xT0"], 16)
            x_copy(Step(0, 2, 0, True))
            x_copy(Step(0, 2, 1, True))

            ac.wait_ge(ld["small"], 16)
            act(expA[:], sm("A_log"), ACT.Exp).then_inc(s0a, 1)
            ac.wait_ge(s0v, 2)
            act(dte[:], dta[:], ACT.Exp).then_inc(s0a, 1)
            ac.wait_ge(s0a, 2)
            ac.wait_ge(ld["cst"], 16)
            act(dtl[:], dte[:], ACT.Ln, bias=c("ones")[:, 0:1]).then_inc(s0a, 1)
            ac.wait_ge(dec_mm, 1)
            act(fC[:].rearrange("p t h -> p (t h)"), bank[3][:, 0:256], ACT.Exp).then_inc(s0a, 1)
            act(fE[:], bank[3][:, 0:256], ACT.Exp, scale=-1.0).then_inc(s0a, 1)
            ac.wait_ge(s0v, 7)
            act(gx[:], gs[:], ACT.Exp, scale=0.5).then_inc(s0a, 1)
            for g in range(4):
                ac.wait_ge(z_mm, g + 1)
                act(sil_all[:, g * 4:(g + 1) * 4, :].rearrange("p t d -> p (t d)"), bank[Z_BANKS[g]][:, :],
                    ACT.Silu).then_inc(sil_act, 1)

            def x2_keep(t):
                ac.wait_ge(s1["x2_dve"], t.count())
                act(x2_all[:, bass.ds(t.val(), 1), :].rearrange("p o d -> p (o d)"), x2[t.slot(2)][:],
                    cp).then_inc(s1["x2k_act"], 1)

            def cb_copy(t):
                if t.had(2):
                    ac.wait_ge(s1["yc_mm"], t.back(2).count())
                    ac.wait_ge(s1["sc1_mm"], t.back(2).count())
                if t.peeled and t.off == 0:
                    ac.wait_ge(gm_done, 1)
                ac.wait_ge(s1["cbt_mm"], t.count())
                act(cb[t.slot(2)][:].rearrange("p k t -> p (k t)"), bank[2][:, :], cp).then_inc(s1["cb_act"], 1)

            def block_diag(t):
                b = t.slot(2)
                if t.had(2):
                    ac.wait_ge(s1["sc1_mm"], t.back(2).count())
                for h in range(HH):
                    m = act(cbd[b][:, :, :, h * Q:(h + 1) * Q],
                            bank[2][:, 0:2 * P].rearrange("p (j q i) -> p j q i", j=2, q=NC), cp, scale=c("head8")[:, h:h + 1])
                m.then_inc(s1["bd_act"], 1)

            def yT_copy(t):
                ac.wait_ge(s1["yt_mm"], t.count())
                if t.had(2):
                    ac.wait_ge(s1["wo_mm"], t.back(2).count())
                act(yT[t.slot(2)][:], bank[6][:, 0:P], cp).then_inc(s1["yt_act"], 1)

            def square(t):
                b = t.slot(2)
                ac.wait_ge(s1["y_add"], t.count())
                if t.had(2):
                    ac.wait_ge(s1["ms_dve"], t.back(2).count())
                act(ysq[b][:], yr[b][:], ACT.Square, accum_out=ss[b][:, 0:1]).then_inc(s1["sq_act"], 1)

            def take_b(t):
                b = t.slot(2)
                ac.wait_ge(s1["xz_dve"], t.count())
                if t.had(2):
                    ac.wait_ge(s1["st_mm"], t.back(2).count())
                act(bs[b][:], bank[b][:, 128:384], cp).then_inc(s1["b_act"], 1)

            def row_copy(t):
                b = t.slot(2)
                ac.wait_ge(s1["x2k_act"], t.count())
                if t.had(2):
                    for k in range(TOPK):
                        ac.wait_ge(sent[k][b], t.back(2).dma(2))
                act(rows[b][:, 0:D], x2_all[:, bass.ds(t.val(), 1), :].rearrange("p o d -> p (o d)"),
                    cp).then_inc(s1["row_act"], 1)

            def x2_copy(t):
                b = t.slot(2)
                ac.wait_ge(s1["x2t_mm"], t.count())
                if t.had(2):
                    ac.wait_ge(s1["lg_mm"], t.back(2).count())
                    ac.wait_ge(s1["lg_dve"], t.back(2).count())
                act(x2T[b][:], bank[6][:, P:2 * P], cp).then_inc(s1["x2t_act"], 1)
                act(x2sq[b][:], x2[b][:], ACT.Square, accum_out=xsq[b][:, 0:1]).then_inc(s1["x2c_act"], 1)

            def gate_exp(t):
                b = t.slot(2)
                ac.wait_ge(s1["gate_dve"], t.count())
                if t.had(2):
                    ac.wait_ge(s1["c_rb"], t.back(2).val(5, 5))
                act(ge[b][:], v8[b][:, 0:TOPK], ACT.Exp, bias=nv[b][:, 0:1], accum_out=gsum[b][:, 0:1]).then_inc(s1["ge_act"], 1)

            def step(s):
                for fn, lag in ((square, 3), (take_b, 1), (gate_exp, 6), (x_copy, -2), (cb_copy, 0),
                                (row_copy, 6), (block_diag, 0), (yT_copy, 3), (x2_copy, 4), (x2_keep, 4)):
                    if s.back(lag).live(NT):
                        fn(s.back(lag))

            run_steps(ac, step, NT - 2, 2, LO1, N1)

            act(warm[:], c("ones")[:, 0:1], ACT.Gelu)

            def bt_copy(b):
                ac.wait_ge(s3["bt_mm"], b.count())
                if b.had(2):
                    ac.wait_ge(s3["h_mm"], b.back(2).count())
                act(xbT[b.slot(2)][:], bank[0][:, 0:P], cp).then_inc(s3["bt_act"], 1)

            def gelu(b):
                u, w = b.slot(2), w1c[b.slot(RB)]
                ac.wait_ge(s3["h_mm"], b.count())
                if b.had(2):
                    ac.wait_ge(s3["yb_mm"], b.back(2).count())
                for f in range(FB):
                    m = act(hT[u][:, f * P:(f + 1) * P], bank[1 + u][:, f * P:(f + 1) * P], ACT.Gelu,
                            bias=w[:, F + f:F + f + 1])
                m.then_inc(s3["ht_act"], 1)

            def weigh(b):
                u, r = b.slot(2), b.slot(RB)
                ac.wait_ge(s3["yb_dve"], b.count())
                ac.wait_ge(s3["gt_dve"], b.count())
                if b.had(RB):
                    ac.wait_ge(put[r], b.back(RB).dma(RB))
                act(yw[r][:], yb[u][:], cp, scale=gt[r][:, 0:1]).then_inc(s3["yw_act"], 1)

            def step3(s):
                for fn, lag in ((bt_copy, -1), (gelu, 0), (weigh, 2)):
                    if s.back(lag).live(NBLK):
                        fn(s.back(lag))

            bt_copy(Step(0, 4, 0, True))
            run_steps(ac, step3, NBLK - 4, 4, LO3, N3)

            for g in range(NG):
                ac.wait_ge(sf["sh_fin"], g + 1)
                for t in range(GT):
                    at_t = g * GT + t
                    m = act(o4[g][:, t, :], bank[g][:, t * D:(t + 1) * D], ACT.Identity, scale=rv4[:, at_t:at_t + 1],
                            bias=sh4[:, at_t:at_t + 1])
                m.then_inc(sf["o_fin"], 1)
                ac.wait_ge(sf["o_fin"], g + 1)
                ac.dma_start(d["out"].rearrange("(g t p) d -> g p t d", g=NG, t=GT)[g], o4[g]).then_inc(oout, 16)
            ac.wait_ge(oout, 16 * NG)

        @block.gpsimd
        def _(po):
            po.wait_ge(ld["cst"], 16)
            mhalf = c("mhalf")[:, 0:1]

            def power(src, dst, ready, done, t):
                po.wait_ge(ready, t.count())
                po.tensor_tensor(dst[t.slot(2)][:], src[t.slot(2)][:], mhalf, ALU.pow).then_inc(done, 1)

            def pow_rms(t):
                if t.had(2):
                    po.wait_ge(s1["yg_dve"], t.back(2).count())
                power(ms, rs, s1["ms_dve"], s1["pow1"], t)

            def pow_ln(t):
                if t.had(2):
                    po.wait_ge(s1["x2_dve"], t.back(2).count())
                power(vre, rv, s1["ve_dve"], s1["pow2"], t)

            def send(t):
                b = t.slot(2)
                wait_apart(po, [(s1["slot_dve"], t.count()), (s1["row_act"], t.count())], zero_out, 16)
                for k in range(TOPK):
                    po.indirect_dma_start(out=xrows, out_offset=bass.IndirectOffsetOnAxis(ap=sli[b][:, k:k + 1], axis=0),
                                          in_=rows[b][:, :], in_offset=None).then_inc(sent[k][b], 16)

            def step(s):
                for fn, lag in ((pow_rms, 3), (pow_ln, 4), (send, 6)):
                    if s.back(lag).live(NT):
                        fn(s.back(lag))

            po.wait_ge(zero_out, 16)
            run_steps(po, step, NT, 2, LO1, N1)

            def give(b):
                r = b.slot(RB)
                wait_apart(po, [(s3["yw_act"], b.count()), (s3["id_dve"], b.count())], zero_out, 16)
                po.indirect_dma_start(out=yrows, out_offset=bass.IndirectOffsetOnAxis(ap=idi[r][:, 0:1], axis=0),
                                      in_=yw[r][:, :], in_offset=None, bounds_check=S * TOPK - 1,
                                      oob_is_err=False).then_inc(put[r], 16)

            run_steps(po, give, NBLK, 4, LO3, NBLK)

            for g in range(NG):
                r = slice(g * GT, (g + 1) * GT)
                po.wait_ge(sf["ve_fin"], g + 1)
                po.tensor_tensor(rv4[:, r], ve4[:, r], c("mhalf"), ALU.pow).then_inc(sf["pow_fin"], 1)


_OUT = ((1, 2048, 128), "float32")


def kernel(**inputs):
    import numpy as _np
    import concourse.bacc as _bacc
    from concourse import mybir as _mybir
    from concourse.bass_utils import run_bass_kernel_spmd as _run

    a = {k: _np.asarray(v) for k, v in inputs.items()}
    x = a["L0_attn_x"][0]
    win = a["L0_attn_W_in"]

    def rep(v):
        return _np.broadcast_to(v[None, :], (P, v.shape[0]))

    def flat(v):
        return _np.ascontiguousarray(v)

    host = {
        "consts": const_table()[1],
        "dtlow": flat(_np.concatenate([win[768:784], a["L0_attn_dt_W"].T], 1)),
        "small": flat(_np.concatenate([rep(a["L0_attn_dt_b"]), rep(a["L0_attn_A_log"]), rep(a["L0_attn_D_param"]),
                                       rep(a["L0_ffn_rb"]), a["L0_attn_norm_w"][:, None]], 1)),
        "xT": flat(x.T),
        "x": flat(x.reshape(NT, P, D).transpose(1, 0, 2)),
        "winT": flat(_np.concatenate([win[0:128], win[256:768], win[128:256]]).T),
        "woutT": flat(a["L0_attn_W_out"].T),
        "kT": flat(_np.stack([a["L0_ffn_keys"].T, a["L0_ffn_rw"].T], 1)),
        "w1T": flat(_np.concatenate([a["L0_ffn_w1"].transpose(2, 0, 1),
                                     a["L0_ffn_b1"].reshape(E, FB, P).transpose(2, 0, 1)], 2)),
        "w2T": flat(a["L0_ffn_w2"].transpose(2, 0, 1).reshape(FB, P, E, D).transpose(1, 2, 0, 3)),
        "b2": flat(a["L0_ffn_b2"].reshape(-1)),
    }
    nc = _bacc.Bacc("TRN2", target_bir_lowering=False, num_devices=1)
    d = {n: nc.dram_tensor(f"in_{n}", v.shape, _mybir.dt.from_np(v.dtype), kind="ExternalInput").ap() for n, v in host.items()}
    d["out"] = nc.dram_tensor("out_0", (S, D), F32, kind="ExternalOutput").ap()
    block_and_moe(nc, d)
    r = _run(nc, [{f"in_{n}": v for n, v in host.items()}], core_ids=[0])
    return r.results[0]["out_0"].reshape(_OUT[0])
```
